# Optimizing a Trainium2 kernel written in Bass

```python
import numpy as np
import jax
import jax.numpy as jnp

def _softmax(x, axis=-1):
    return jax.nn.softmax(x, axis=axis)

def _gelu(x):
    return jax.nn.gelu(x, approximate=True)

def _silu(x):
    return jax.nn.silu(x)

def _sigmoid(x):
    return jax.nn.sigmoid(x)

def _layernorm(x, axis=-1, eps=1e-05):
    m = jnp.mean(x, axis=axis, keepdims=True)
    v = jnp.var(x, axis=axis, keepdims=True)
    return (x - m) / jnp.sqrt(v + eps)

def _scatter_add(tgt, idx, src, axis=0):
    return tgt.at[idx].add(src)

def _segment_sum(src, seg, n):
    return jax.ops.segment_sum(src, seg, n)
kernel_name = 'mk_perceiver_d1_seqx_r2_20d557'

def setup_inputs(seed: int=0):
    np.random.seed(seed)
    _w = jnp.asarray

    def _rec_inputs():
        import jax
        import jax.numpy as jnp
        _rk = jax.random.key(seed)
        x = -0.0002928 + 1 * jax.random.normal(jax.random.fold_in(_rk, 1), (128, 32, 512), jnp.float32)
        _lenS = 32 - jax.random.randint(jax.random.fold_in(_rk, 7), (128,), 0, max(1, 32 // 4) + 1, jnp.int32)
        _lenS2 = 257 - jax.random.randint(jax.random.fold_in(_rk, 8), (128,), 0, max(1, 257 // 4) + 1, jnp.int32)
        _ctx_1024P = jax.random.normal(jax.random.fold_in(_rk, 11), (128, 16, 512), jnp.float32)
        _ctx_1024c = jax.random.dirichlet(jax.random.fold_in(_rk, 511), 0.3 * jnp.ones((16,), jnp.float32), (128, 257))
        _ctx_1024t = jnp.einsum('bsk,bkd->bsd', _ctx_1024c, _ctx_1024P)
        _ctx_1024t = _ctx_1024t * jax.lax.rsqrt(jnp.mean(jnp.square(_ctx_1024t)) + 1e-12) * 0.953939
        ctx_1024 = -1.39393e-06 + 0.999914 * (_ctx_1024t + 0.3 * jax.random.normal(jax.random.fold_in(_rk, 611), (128, 257, 512), jnp.float32))
        _validS = jnp.arange(32)[None, :] < _lenS[:, None]
        _validS2 = jnp.arange(257)[None, :] < _lenS2[:, None]
        _causal = jnp.tril(jnp.ones((32, 32), dtype=bool))
        mask_BxSxS2_ik0 = jnp.where(jnp.broadcast_to(_validS2[:, None, :], (128, 32, 257)), 0, 1).astype(jnp.int32)
        return (x, ctx_1024, mask_BxSxS2_ik0)
    x, ctx_1024, mask_BxSxS2_ik0 = _rec_inputs()

    def _L0_xattn_setup():
        import jax, jax.numpy as jnp
        import numpy as np
        import math
        B, S, D, H = (2, 1024, 512, 16)
        DK = D // H

        def _split_heads(x):
            b, s, _ = x.shape
            return x.reshape(b, s, H, DK).transpose(0, 2, 1, 3)
        key = jax.random.key(seed)
        ks = jax.random.split(key, 12)
        s = 1.0 / math.sqrt(D)
        inp = {'query': jax.random.normal(ks[0], (B, S, D), jnp.float32), 'key': jax.random.normal(ks[1], (B, S, D), jnp.float32), 'value': jax.random.normal(ks[2], (B, S, D), jnp.float32), 'mask': jnp.tril(jnp.ones((S, S), jnp.int32))[None].repeat(B, axis=0), 'Wq': jax.random.normal(ks[3], (D, D), jnp.float32) * s, 'bq': jnp.zeros((D,), jnp.float32), 'Wk': jax.random.normal(ks[4], (D, D), jnp.float32) * s, 'bk': jnp.zeros((D,), jnp.float32), 'Wv': jax.random.normal(ks[5], (D, D), jnp.float32) * s, 'bv': jnp.zeros((D,), jnp.float32), 'Wo': jax.random.normal(ks[6], (D, D), jnp.float32) * s, 'bo': jnp.zeros((D,), jnp.float32)}
        return inp
    _L0_xattn_all = _L0_xattn_setup()
    _L0_xattn_in = {k: v for k, v in _L0_xattn_all.items() if k in ('Wq', 'bq', 'Wk', 'bk', 'Wv', 'bv', 'Wo', 'bo')}
    del _L0_xattn_all

    def _L0_attn_setup():
        import jax, jax.numpy as jnp
        import numpy as np
        B, T, D, H = (1, 2048, 512, 16)
        DK = D // H
        SCALE = 1.0 / float(np.sqrt(DK))
        NEG = -1000000000.0
        key = jax.random.key(seed)
        k1, k2, k3 = jax.random.split(key, 3)
        x = jax.random.normal(k1, (B, T, D), dtype=jnp.float32)
        Wqkv = jax.random.normal(k2, (3 * D, D), dtype=jnp.float32) * 0.02
        Wout = jax.random.normal(k3, (D, D), dtype=jnp.float32) * 0.02
        return {'x': x, 'Wqkv': Wqkv, 'Wout': Wout}
    _L0_attn_all = _L0_attn_setup()
    _L0_attn_in = {k: v for k, v in _L0_attn_all.items() if k in ('Wqkv', 'Wout')}
    del _L0_attn_all

    def _L0_ffn_setup():
        import jax, jax.numpy as jnp
        import numpy as np
        NUM_OPS, B, T, D = (8, 8, 256, 512)
        key = jax.random.key(seed)
        k1, k2, k3, k4 = jax.random.split(key, 4)
        x = jax.random.normal(k1, (B, T, D), dtype=jnp.float32)
        W = jax.random.normal(k2, (NUM_OPS, D, D), dtype=jnp.float32) * 0.02
        b = jnp.zeros((NUM_OPS, D), dtype=jnp.float32)
        logits = 0.001 * jax.random.normal(k3, (NUM_OPS,), dtype=jnp.float32)
        u = jax.random.uniform(k4, (NUM_OPS,), dtype=jnp.float32, minval=1e-06, maxval=1.0 - 1e-06)
        return {'x': x, 'W': W, 'b': b, 'logits': logits, 'u': u}
    _L0_ffn_all = _L0_ffn_setup()
    _L0_ffn_in = {k: v for k, v in _L0_ffn_all.items() if k in ('W', 'b', 'logits', 'u')}
    del _L0_ffn_all
    return {'x': x, 'ctx_1024': ctx_1024, 'mask_BxSxS2_ik0': mask_BxSxS2_ik0, 'L0_xattn_Wq': _L0_xattn_in['Wq'], 'L0_xattn_bq': _L0_xattn_in['bq'], 'L0_xattn_Wk': _L0_xattn_in['Wk'], 'L0_xattn_bk': _L0_xattn_in['bk'], 'L0_xattn_Wv': _L0_xattn_in['Wv'], 'L0_xattn_bv': _L0_xattn_in['bv'], 'L0_xattn_Wo': _L0_xattn_in['Wo'], 'L0_xattn_bo': _L0_xattn_in['bo'], 'L0_attn_Wqkv': _L0_attn_in['Wqkv'], 'L0_attn_Wout': _L0_attn_in['Wout'], 'L0_ffn_W': _L0_ffn_in['W'], 'L0_ffn_b': _L0_ffn_in['b'], 'L0_ffn_logits': _L0_ffn_in['logits'], 'L0_ffn_u': _L0_ffn_in['u']}

def reference(x, ctx_1024, mask_BxSxS2_ik0, L0_xattn_Wq, L0_xattn_bq, L0_xattn_Wk, L0_xattn_bk, L0_xattn_Wv, L0_xattn_bv, L0_xattn_Wo, L0_xattn_bo, L0_attn_Wqkv, L0_attn_Wout, L0_ffn_W, L0_ffn_b, L0_ffn_logits, L0_ffn_u):
    import jax
    import jax.numpy as jnp

    def _L0_xattn_ref(query, key, value, mask, Wq, bq, Wk, bk, Wv, bv, Wo, bo):
        import jax, jax.numpy as jnp
        import numpy as np
        import math
        B, S, D, H = (2, 1024, 512, 16)
        DK = D // H

        def _split_heads(x):
            b, s, _ = x.shape
            return x.reshape(b, s, H, DK).transpose(0, 2, 1, 3)
        q = _split_heads(query @ Wq + bq)
        k = _split_heads(key @ Wk + bk)
        v = _split_heads(value @ Wv + bv)
        scores = jnp.einsum('bhqd,bhkd->bhqk', q, k) / math.sqrt(DK)
        scores = jnp.where(mask[:, None, :, :] == 0, jnp.float32(-1000000000.0), scores)
        p = jax.nn.softmax(scores, axis=-1)
        x = jnp.einsum('bhqk,bhkd->bhqd', p, v)
        x = x.transpose(0, 2, 1, 3).reshape(query.shape[0], -1, D)
        return x @ Wo + bo

    def _L0_attn_ref(x, Wqkv, Wout):
        import jax, jax.numpy as jnp
        import numpy as np
        B, T, D, H = (1, 2048, 512, 16)
        DK = D // H
        SCALE = 1.0 / float(np.sqrt(DK))
        NEG = -1000000000.0
        b, t, d = x.shape
        qkv = jnp.einsum('btd,ed->bte', x, Wqkv)
        qkv = qkv.reshape(b, t, 3, H, DK).transpose(2, 0, 3, 1, 4)
        q, k, v = (qkv[0], qkv[1], qkv[2])
        scores = jnp.einsum('bhtd,bhsd->bhts', q, k) * SCALE
        scores = jnp.clip(scores, -10.0, 10.0)
        mask = jnp.triu(jnp.full((t, t), NEG, dtype=scores.dtype), k=1)
        scores = scores + mask[None, None, :, :]
        attn = jax.nn.softmax(scores, axis=-1)
        out = jnp.einsum('bhts,bhsd->bhtd', attn, v)
        out = out.transpose(0, 2, 1, 3).reshape(b, t, d)
        return jnp.einsum('btd,ed->bte', out, Wout)

    def _L0_ffn_ref(x, W, b, logits, u):
        import jax, jax.numpy as jnp
        import numpy as np
        NUM_OPS, B, T, D = (8, 8, 256, 512)
        gumbel = -jnp.log(-jnp.log(u))
        idx = jnp.argmax(jax.nn.log_softmax(logits) + gumbel)
        out = jnp.einsum('btd,de->bte', x, W[idx]) + b[idx]
        return out
    x = x + _L0_xattn_ref(_layernorm(x, axis=-1), ctx_1024, ctx_1024, mask_BxSxS2_ik0, L0_xattn_Wq, L0_xattn_bq, L0_xattn_Wk, L0_xattn_bk, L0_xattn_Wv, L0_xattn_bv, L0_xattn_Wo, L0_xattn_bo)
    x = x + _L0_attn_ref(_layernorm(x, axis=-1), L0_attn_Wqkv, L0_attn_Wout)
    x = x + _L0_ffn_ref(_layernorm(x, axis=-1), L0_ffn_W, L0_ffn_b, L0_ffn_logits, L0_ffn_u)
    return x

_drawn_inputs = setup_inputs


def setup_inputs(seed=0):
    import zlib

    import numpy as np

    out = dict(_drawn_inputs(seed))
    spreads = {'L0_xattn_bq': (0.0, 0.343),
     'L0_xattn_bk': (0.0, 0.8),
     'L0_xattn_bv': (0.0, 0.1),
     'L0_xattn_bo': (0.0, 0.1),
     'L0_ffn_b': (0.0, 0.1)}
    factors = {}
    for name, (base, spread) in spreads.items():
        noise = np.random.default_rng([zlib.crc32(name.encode()), seed]).standard_normal(out[name].shape)
        drawn = base * np.exp(spread * noise) if base else spread * noise
        out[name] = jnp.asarray(drawn.astype(out[name].dtype))
    for name, factor in factors.items():
        out[name] = (out[name] * factor).astype(out[name].dtype)
    return out
```

```python
from contextlib import ExitStack

import concourse.bass as bass
from concourse import mybir

F32 = mybir.dt.float32
F32R = mybir.dt.float32r
I32 = mybir.dt.int32
U32 = mybir.dt.uint32
ALU = mybir.AluOpType
ACT = mybir.ActivationFunctionType
AX = mybir.AxisListType

P = 128
B, S, D, H = 128, 32, 512, 16
DK = D // H
KEYS = 257
NK = KEYS - 1
C = D // P
HG = P // DK
TOK = B * S
SUP = 512
NSUP = TOK // SUP
TILES = SUP // P
PAIRS = B // 2
QUADS = B // 4
OPS = 8
SCALE = float(DK) ** -0.5
EPS = 1e-5
MASKED = -1e30
FAR = 3.0e38


def wait(eng, sem, value):
    if not (isinstance(value, int) and value <= 0):
        eng.wait_ge(sem, value)


def product3(eng, out, w_hi, w_lo, m_hi, m_lo):
    last = None
    for c in range(C):
        for k, (w, m) in enumerate(((w_hi, m_hi), (w_hi, m_lo), (w_lo, m_hi))):
            last = eng.matmul(out, w(c), m(c), start=(c == 0 and k == 0), stop=(c == C - 1 and k == 2))
    return last


def normalise(dve, x, xn, stats, mv, small, gate, var_ready, seed_ready, done, step_sem, base, n):
    for t in range(TILES):
        i = dve.bn_stats(stats[:, t, :], x[:, t, :])
    i.then_inc(step_sem, 1)
    dve.wait_ge(step_sem, base + 1)
    dve.memset(gate, 0.0)
    for t in range(TILES):
        i = dve.bn_aggr(mv[:, t, :], stats[:, t, :])
    i.then_inc(step_sem, 1)
    dve.wait_ge(step_sem, base + 2)
    dve.tensor_scalar(small[:, 0, :], mv[:, :, 1], EPS, None, ALU.add).then_inc(var_ready, 1)
    dve.wait_ge(seed_ready, n + 1)
    dve.tensor_tensor(small[:, 2, :], small[:, 1, :], small[:, 1, :], ALU.mult).then_inc(step_sem, 1)
    dve.wait_ge(step_sem, base + 3)
    dve.tensor_tensor(small[:, 2, :], small[:, 2, :], small[:, 0, :], ALU.mult).then_inc(step_sem, 1)
    dve.wait_ge(step_sem, base + 4)
    dve.tensor_scalar(small[:, 2, :], small[:, 2, :], -0.5, 1.5, ALU.mult, ALU.add).then_inc(step_sem, 1)
    dve.wait_ge(step_sem, base + 5)
    dve.tensor_tensor(small[:, 1, :], small[:, 1, :], small[:, 2, :], ALU.mult).then_inc(step_sem, 1)
    dve.wait_ge(step_sem, base + 6)
    for t in range(TILES):
        i = dve.tensor_scalar(xn[:, t, :], x[:, t, :], mv[:, t, 0:1], small[:, 1, t:t + 1],
                              ALU.subtract, ALU.mult)
    i.then_inc(done, 1)


LN_STEPS = 6


def rsqrt_seed(act, small, var_ready, half_sem, seed_ready, n):
    act.wait_ge(var_ready, n + 1)
    act.activation(small[:, 3, :], small[:, 0, :], ACT.Ln).then_inc(half_sem, 1)
    act.wait_ge(half_sem, n + 1)
    act.activation(small[:, 1, :], small[:, 3, :], ACT.Exp, scale=-0.5).then_inc(seed_ready, 1)


def phase_a(nc, io, w, scr):
    with ExitStack() as ctx:
        def sb(name, shape, dt=F32):
            return ctx.enter_context(nc.sbuf_tensor("a_" + name, shape, dt))

        def sem(name):
            return ctx.enter_context(nc.semaphore("a_" + name))

        raw = sb("raw", [P, 4, C, D])
        wq_hi = sb("wq_hi", [P, C, D], F32R)
        wq_lo = sb("wq_lo", [P, C, D], F32R)
        last_t = sb("last_t", [P, C, B])
        bq = sb("bq", [P, C])
        bqs = sb("bqs", [P, C])
        bv = sb("bv", [P, C])
        x = sb("x", [P, 2, TILES, D])
        xt_hi = sb("xt_hi", [P, C, SUP], F32R)
        xt_lo = sb("xt_lo", [P, C, SUP], F32R)
        q = sb("q", [P, SUP // 64, C, 64])
        stats = sb("stats", [P, TILES, 6])
        mv = sb("mv", [P, TILES, 2])
        small = sb("small", [P, 4, TILES])
        gate = sb("gate", [1, 1])
        pick = sb("pick", [1, 8, OPS])
        best = sb("best", [1, OPS])
        ps = ctx.enter_context(nc.psum_tensor("a_ps", [P, 8, 512], F32))
        PROJ, TRN, VL = (0, 1), (2, 3), 4

        weights_in = [sem(f"weights_in{k}") for k in range(4)]
        consts_in, last_in, pick_in = sem("consts_in"), sem("last_in"), sem("pick_in")
        pick_act, pick_dve = sem("pick_act"), sem("pick_dve")
        x_in = [sem("x_in0"), sem("x_in1")]
        hi_done, lo_done = sem("hi_done"), sem("lo_done")
        bqs_done = sem("bqs_done")
        vl_mm, vl_done = sem("vl_mm"), sem("vl_done")
        var_ready, half, seed_ready = sem("var_ready"), sem("half"), sem("seed_ready")
        step_sem, xn_done = sem("ln_step"), sem("xn_done")
        transposed = sem("transposed")
        xt_hi_done, xt_lo_done = sem("xt_hi_done"), sem("xt_lo_done")
        q_mm, q_evac = sem("q_mm"), sem("q_evac")
        q_stored = sem("q_stored")
        block = ctx.enter_context(nc.Block())
        hi = (wq_hi, w["wk_hi"], w["wv_hi"], w["wo_hi"])
        lo = (wq_lo, w["wk_lo"], w["wv_lo"], w["wo_lo"])

        @block.sync
        def _(sp):
            def load(s, par):
                wait(sp, transposed, 4 * (s - 1))
                sp.dma_start(x[:, par], io["x"][s].rearrange("t p n -> p t n")).then_inc(x_in[par], 16)

            def store(s):
                sp.wait_ge(q_evac, s * 4 + 4)
                sp.dma_start(scr["q"][s].rearrange("a p n -> p a n"),
                             q[:].rearrange("p a g t -> p a (g t)")).then_inc(q_stored, 16)

            load(0, 0)
            names = ("Wq", "Wk", "Wv", "Wo")
            sp.dma_start(raw[:, 0], io["Wq"]).then_inc(weights_in[0], 16)
            sp.dma_start(bq[:], io["bq"]).then_inc(consts_in, 16)
            sp.dma_start(bv[:], io["bv"]).then_inc(consts_in, 16)
            sp.dma_start(w["bk"][:], io["bk"]).then_inc(consts_in, 16)
            load(1, 1)
            for k in (2, 1, 3):
                sp.dma_start(raw[:, k], io[names[k]]).then_inc(weights_in[k], 16)
            sp.dma_start(last_t[:], io["ctx_last"]).then_inc(last_in, 16)
            sp.dma_start(pick[:, 0, :], io["logits"]).then_inc(pick_in, 16)
            sp.dma_start(pick[:, 1, :], io["u"]).then_inc(pick_in, 16)
            load(2, 0)
            store(0)
            load(3, 1)
            store(1)
            with sp.Fori(1, NSUP // 2 - 1) as i:
                for par in range(2):
                    load(i * 2 + (2 + par), par)
                    store(i * 2 + par)
            store(NSUP - 2)
            store(NSUP - 1)
            sp.wait_ge(q_stored, 16 * NSUP)

        @block.scalar
        def _(act):
            def seed(s):
                rsqrt_seed(act, small, var_ready, half, seed_ready, s)

            def step(s, more):
                for c in range(C):
                    act.wait_ge(transposed, s * 4 + (c + 1))
                    if c == 0:
                        wait(act, q_mm, s * 4)
                    act.copy(xt_hi[:, c, :], ps[:, TRN[c % 2], :]).then_inc(xt_hi_done, 1)
                if more:
                    seed(s + 1)
                for g in range(C):
                    act.wait_ge(q_mm, s * 4 + (g + 1))
                    if g == 0:
                        wait(act, q_stored, 16 * s)
                    act.activation(q[:, :, g, :], ps[:, PROJ[g % 2], :].rearrange("p (a t) -> p a t", t=64),
                                   ACT.Identity, bias=bqs[:, g:g + 1], scale=SCALE).then_inc(q_evac, 1)

            seed(0)
            act.wait_ge(weights_in[0], 16)
            act.copy(hi[0][:], raw[:, 0]).then_inc(hi_done, 1)
            act.wait_ge(bqs_done, 1)
            step(0, True)
            step(1, True)
            for k in (2, 1, 3):
                act.wait_ge(weights_in[k], 16)
                act.copy(hi[k][:], raw[:, k]).then_inc(hi_done, 1)
            act.wait_ge(pick_in, 32)
            act.activation(pick[:, 6, :], pick[:, 1, :], ACT.Ln).then_inc(pick_act, 1)
            act.wait_ge(pick_act, 1)
            act.activation(pick[:, 1, :], pick[:, 6, :], ACT.Ln, scale=-1.0).then_inc(pick_act, 1)
            act.wait_ge(pick_dve, 2)
            act.activation(pick[:, 4, :], pick[:, 0, :], ACT.Exp, bias=pick[:, 3, 0:1],
                           accum_out=pick[:, 5, 0:1]).then_inc(pick_act, 1)
            act.wait_ge(pick_act, 3)
            act.activation(pick[:, 6, 0:1], pick[:, 5, 0:1], ACT.Ln).then_inc(pick_act, 1)
            with act.Fori(2, NSUP - 1) as s:
                step(s, True)
            step(NSUP - 1, False)

        @block.vector
        def _(dve):
            def ln(s, par):
                dve.wait_ge(x_in[par], 16 * (s // 2 + 1))
                normalise(dve, x[:, par], x[:, par], stats, mv, small, gate[:], var_ready, seed_ready,
                          xn_done, step_sem, s * LN_STEPS, s)

            def lows(s):
                for c in range(C):
                    dve.wait_ge(xt_hi_done, s * 4 + (c + 1))
                    dve.tensor_tensor(xt_lo[:, c, :], ps[:, TRN[c % 2], :], xt_hi[:, c, :].bitcast(F32),
                                      ALU.subtract).then_inc(xt_lo_done, 1)

            def split_low(k, n):
                dve.wait_ge(hi_done, n)
                dve.tensor_tensor(lo[k][:], raw[:, k], hi[k][:].bitcast(F32), ALU.subtract).then_inc(lo_done, 1)

            ln(0, 0)
            dve.wait_ge(consts_in, 48)
            dve.tensor_scalar(bqs[:], bq[:], SCALE, None, ALU.mult).then_inc(bqs_done, 1)
            split_low(0, 1)
            lows(0)
            ln(1, 1)
            lows(1)
            ln(2, 0)
            for n, k in enumerate((2, 1, 3)):
                split_low(k, n + 2)
            dve.wait_ge(vl_mm, 1)
            for g in range(C):
                i = dve.tensor_scalar(w["v_last"][:, :, g], ps[:, VL, g * B:(g + 1) * B], bv[:, g:g + 1],
                                      None, ALU.add)
            i.then_inc(vl_done, 1)
            dve.wait_ge(pick_in, 32)
            dve.tensor_reduce(pick[:, 2, 0:1], pick[:, 0, :], AX.X, ALU.max).then_inc(pick_dve, 1)
            dve.wait_ge(pick_dve, 1)
            dve.tensor_scalar(pick[:, 3, 0:1], pick[:, 2, 0:1], -1.0, None, ALU.mult).then_inc(pick_dve, 1)
            dve.wait_ge(pick_act, 4)
            dve.tensor_scalar(pick[:, 7, :], pick[:, 0, :], pick[:, 2, 0:1], pick[:, 6, 0:1], ALU.subtract,
                              ALU.subtract).then_inc(pick_dve, 1)
            dve.wait_ge(pick_dve, 3)
            dve.tensor_tensor(pick[:, 4, :], pick[:, 7, :], pick[:, 1, :], ALU.subtract).then_inc(pick_dve, 1)
            dve.wait_ge(pick_dve, 4)
            dve.max(best[:], pick[:, 4, :]).then_inc(pick_dve, 1)
            dve.wait_ge(pick_dve, 5)
            dve.max_index(w["choice"][:], best[:], pick[:, 4, :]).then_inc(pick_dve, 1)
            lows(2)
            with dve.Fori(1, NSUP // 2 - 1) as i:
                for par in (1, 0):
                    s = i * 2 + (2 - par)
                    dve.wait_ge(x_in[par], i * 16 + (2 - par) * 16)
                    normalise(dve, x[:, par], x[:, par], stats, mv, small, gate[:], var_ready, seed_ready,
                              xn_done, step_sem, s * LN_STEPS, s)
                    lows(s)
            ln(NSUP - 1, 1)
            lows(NSUP - 1)

        @block.tensor
        def _(pe):
            def step(s, par):
                pe.wait_ge(xn_done, s + 1)
                for c in range(C):
                    wait(pe, xt_lo_done, s * 4 + (c - 1))
                    for t in range(TILES):
                        i = pe.transpose(ps[:, TRN[c % 2], t * P:(t + 1) * P], x[:, par, t, c * P:(c + 1) * P],
                                         w["ident"][:])
                    i.then_inc(transposed, 1)
                pe.wait_ge(xt_lo_done, s * 4 + 4)
                for g in range(C):
                    wait(pe, q_evac, s * 4 + (g - 1))
                    product3(pe, ps[:, PROJ[g % 2], :],
                             lambda c: wq_hi[:, c, g * P:(g + 1) * P], lambda c: wq_lo[:, c, g * P:(g + 1) * P],
                             lambda c: xt_hi[:, c, :], lambda c: xt_lo[:, c, :]).then_inc(q_mm, 1)

            pe.wait_ge(w["ident_ready"], 2)
            pe.wait_ge(lo_done, 1)
            step(0, 0)
            step(1, 1)
            pe.wait_ge(weights_in[2], 16)
            pe.wait_ge(last_in, 16)
            for g in range(C):
                for c in range(C):
                    i = pe.matmul(ps[:, VL, g * B:(g + 1) * B], raw[:, 2, c, g * P:(g + 1) * P], last_t[:, c, :],
                                  start=(c == 0), stop=(c == C - 1))
            i.then_inc(vl_mm, 1)
            with pe.Fori(1, NSUP // 2) as i:
                step(i * 2, 0)
                step(i * 2 + 1, 1)

        @block.gpsimd
        def _(pool):
            pool.memset(w["ident"][:], 0.0).then_inc(w["ident_ready"], 1)
            pool.wait_ge(w["ident_ready"], 1)
            pool.affine_select(out=w["ident"][:], in_=w["ident"][:], compare_op=ALU.not_equal, fill=1.0,
                               base=0, pattern=[[-1, P]], channel_multiplier=1).then_inc(w["ident_ready"], 1)


def phase_b(nc, io, w, scr):
    with ExitStack() as ctx:
        def sb(name, shape, dt=F32):
            return ctx.enter_context(nc.sbuf_tensor("b_" + name, shape, dt))

        def sem(name):
            return ctx.enter_context(nc.semaphore("b_" + name))

        raw = sb("raw", [P, 2, 2, C, KEYS])
        cx_hi = sb("cx_hi", [P, 2, C, 2 * NK], F32R)
        cx_lo = sb("cx_lo", [P, 2, C, 2 * NK], F32R)
        kt = sb("kt", [P, 2, C, 2, KEYS])
        v = sb("v", [P, 2, 4, D])
        mask_raw = sb("mask_raw", [P, 2, KEYS], I32)
        mask = sb("mask", [P, 2, 2, KEYS])
        qt = sb("qt", [P, 2, C, 64])
        qb = sb("qb", [P, 2, C, P])
        sm = sb("sm", [P, 2, C, KEYS])
        pr = sb("pr", [P, 2, C, KEYS])
        low = sb("low", [P, 2, C])
        rsum = sb("rsum", [P, 2, C])
        rinv = sb("rinv", [P, 2, C])
        pt = sb("pt", [P, 2, 2, D])
        ot = sb("ot", [P, C, P])
        ot_hi = sb("ot_hi", [P, C, P], F32R)
        ot_lo = sb("ot_lo", [P, C, P], F32R)
        x = sb("x", [P, D])
        x2 = sb("x2", [P, D])
        bo = sb("bo", [P, D])
        gate = sb("gate", [1, 2 * C])
        one = sb("one", [P, 1])
        ps = ctx.enter_context(nc.psum_tensor("b_ps", [P, 8, 512], F32))
        PROJ, SC, PT, OUT = (0, 1), (2, 3, 4), (5, 6), 7

        ctx_in = [sem("ctx_in0"), sem("ctx_in1")]
        q_in = [sem("q_in0"), sem("q_in1")]
        mask_in, x_in, bo_in = sem("mask_in"), sem("x_in"), sem("bo_in")
        zeroed, bk_ready = sem("zeroed"), sem("bk_ready")
        mask_ready, qb_ready = sem("mask_ready"), sem("qb_ready")
        cx_hi_done, cx_done = sem("cx_hi_done"), sem("cx_done")
        proj_mm, proj_evac = sem("proj_mm"), sem("proj_evac")
        sc_mm, masked, exp_done = sem("sc_mm"), sem("masked"), sem("exp_done")
        inv_done, norm_done = sem("inv_done"), sem("norm_done")
        pt_mm, pt_evac = sem("pt_mm"), sem("pt_evac")
        pv_mm, o_done = sem("pv_mm"), sem("o_done")
        ot_hi_done, ot_done = sem("ot_hi_done"), sem("ot_done")
        op_mm, xb_done, x2_done, x2_stored = sem("op_mm"), sem("xb_done"), sem("x2_done"), sem("x2_stored")
        block = ctx.enter_context(nc.Block())

        def bank(g, h, par):
            return SC[(h * C + g + (2 if par else 0)) % 3]

        FIRST, LAST = 1, PAIRS // 2 - 1

        @block.sync
        def _(sp):
            def load_ctx(p, par):
                wait(sp, cx_done, (p - 1) * 2)
                for h in range(2):
                    sp.dma_start(raw[:, par, h], io["ctx"][p * 2 + h]).then_inc(ctx_in[par], 16)

            def load_small(p, par):
                wait(sp, mask_ready, p)
                for j in range(HG):
                    sp.dma_start(mask_raw[j * S:(j + 1) * S], io["mask"][p]).then_inc(mask_in, 16)
                wait(sp, qb_ready, (p - 1) * 8)
                sp.dma_start(qt[:, par], scr["q_pairs"][p]).then_inc(q_in[par], 16)

            def quad_io(k):
                wait(sp, x2_done, k)
                sp.dma_start(x[:], io["x_tiles"][k]).then_inc(x_in, 16)
                sp.wait_ge(x2_done, k + 1)
                sp.dma_start(scr["x2"][k], x2[:]).then_inc(x2_stored, 16)

            sp.dma_start(bo[:], io["bo"].partition_broadcast(P)).then_inc(bo_in, 16)
            load_ctx(0, 0)
            load_small(0, 0)
            load_ctx(1, 1)
            for p in range(3):
                load_ctx(p + 2, p % 2)
                load_small(p + 1, 1 - p % 2)
            quad_io(0)
            with sp.Fori(FIRST, LAST - 1) as i:
                load_ctx(i * 2 + 3, 1)
                load_small(i * 2 + 2, 0)
                load_ctx(i * 2 + 4, 0)
                load_small(i * 2 + 3, 1)
                quad_io(i)
            load_ctx(PAIRS - 1, 1)
            load_small(PAIRS - 2, 0)
            load_small(PAIRS - 1, 1)
            quad_io(QUADS - 2)
            quad_io(QUADS - 1)
            sp.wait_ge(x2_stored, 16 * QUADS)

        @block.gpsimd
        def _(pool):
            def expand(p, par, h, nth):
                if h == 0:
                    pool.wait_ge(q_in[par], nth * 16)
                wait(pool, sc_mm, (p * 2 + (h - 1)) * 4)
                for j in range(HG):
                    r = slice(j * DK, (j + 1) * DK)
                    pool.tensor_tensor(qb[r, h, :, r], qt[r, par, :, h * S:(h + 1) * S],
                                       one[r].unsqueeze(1).to_broadcast([DK, C, S]), ALU.mult).then_inc(qb_ready, 1)

            pool.memset(qb[:], 0.0).then_inc(zeroed, 1)
            pool.memset(one[:], 1.0).then_inc(zeroed, 1)
            pool.wait_ge(zeroed, 2)
            for p in range(3):
                expand(p, p % 2, 0, p // 2 + 1)
                expand(p, p % 2, 1, p // 2 + 1)
            with pool.Fori(FIRST, LAST) as i:
                for n, par in ((1, 1), (2, 0)):
                    p = i * 2 + n
                    expand(p, par, 0, i + n)
                    expand(p, par, 1, i + n)
            p = PAIRS - 1
            expand(p, 1, 0, PAIRS // 2)
            expand(p, 1, 1, PAIRS // 2)

        @block.scalar
        def _(act):
            def step(p, par, attend=True, project=True, ahead=True):
                def evac(n):
                    if not project:
                        return
                    act.wait_ge(proj_mm, p * 8 + (n + 1))
                    if n < 4:
                        if n == 0:
                            wait(act, sc_mm, (p - 1) * 8)
                        act.activation(kt[:, par, n, :, 0:NK], ps[:, PROJ[n % 2], :].rearrange(
                            "p (h k) -> p h k", h=2), ACT.Identity, bias=w["bk"][:, n:n + 1]).then_inc(proj_evac, 1)
                    else:
                        if n == 4:
                            wait(act, pv_mm, (p - 1) * 2)
                        act.copy(v[:, par, n - 4, :], ps[:, PROJ[n % 2], :]).then_inc(proj_evac, 1)

                def exps(h):
                    if not attend:
                        return
                    b = (p - 1) * 2 + h
                    wait(act, pt_mm, (b - 1) * 2)
                    for g in range(C):
                        act.wait_ge(masked, b * 4 + (g + 1))
                        act.activation(pr[:, h, g, :], sm[:, h, g, :], ACT.Exp, bias=low[:, h, g:g + 1],
                                       scale=-1.0, accum_out=rsum[:, h, g:g + 1]).then_inc(exp_done, 1)

                def pt_out(h):
                    if not attend:
                        return
                    b = (p - 1) * 2 + h
                    for kc in range(2):
                        act.wait_ge(pt_mm, b * 2 + (kc + 1))
                        if kc == 0:
                            wait(act, pv_mm, b - 1)
                        act.copy(pt[:, h, kc, :], ps[:, PT[kc], :]).then_inc(pt_evac, 1)

                evac(0)
                exps(0)
                evac(1)
                exps(1)
                evac(2)
                pt_out(0)
                evac(3)
                pt_out(1)
                evac(4)
                evac(5)
                evac(6)
                evac(7)

            step(0, 0, attend=False)
            step(1, 1)
            step(2, 0)
            with act.Fori(FIRST, LAST) as i:
                step(i * 2 + 1, 1)
                step(i * 2 + 2, 0)
            step(PAIRS - 1, 1)
            step(PAIRS, 0, project=False)

        @block.vector
        def _(dve):
            def split(p, par, h):
                if h == 0:
                    wait(dve, proj_mm, (p - 1) * 8)
                    dve.wait_ge(ctx_in[par], in_count(p))
                for c in range(C):
                    i = dve.tensor_scalar(cx_hi[:, par, c, h * NK:(h + 1) * NK], raw[:, par, h, c, 0:NK],
                                          raw[:, par, h, c, NK:KEYS], None, ALU.subtract)
                i.then_inc(cx_hi_done, 1)
                dve.wait_ge(cx_hi_done, p * 2 + (h + 1))
                for c in range(C):
                    i = dve.scalar_tensor_tensor(cx_lo[:, par, c, h * NK:(h + 1) * NK], raw[:, par, h, c, 0:NK],
                                                 raw[:, par, h, c, NK:KEYS],
                                                 cx_hi[:, par, c, h * NK:(h + 1) * NK].bitcast(F32),
                                                 ALU.subtract, ALU.subtract)
                i.then_inc(cx_done, 1)

            loop = [None]

            def in_count(p):
                return 32 * (p // 2 + 1) if isinstance(p, int) else loop[0] * 32 + 64

            def step(p, par, attend=True, project=True, ahead=True):
                def mask_rows(h):
                    if not attend:
                        return
                    b = (p - 1) * 2 + h
                    if h == 0:
                        dve.wait_ge(mask_ready, p)
                    wait(dve, exp_done, (b - 1) * 4)
                    for g in range(C):
                        dve.wait_ge(sc_mm, b * 4 + (g + 1))
                        dve.memset(gate[:, h * C + g:h * C + g + 1], 0.0)
                        dve.tensor_tensor_reduce(sm[:, h, g, :], ps[:, bank(g, h, par), 0:KEYS],
                                                 mask[:, 1 - par, h, :], -1.0, FAR, ALU.add, ALU.min,
                                                 low[:, h, g:g + 1]).then_inc(masked, 1)

                def norm(h):
                    if not attend:
                        return
                    b = (p - 1) * 2 + h
                    dve.wait_ge(exp_done, b * 4 + 4)
                    dve.reciprocal(rinv[:, h, :], rsum[:, h, :]).then_inc(inv_done, 1)
                    dve.wait_ge(inv_done, b + 1)
                    for g in range(C):
                        i = dve.tensor_scalar(pr[:, h, g, 0:NK], pr[:, h, g, 0:NK], rinv[:, h, g:g + 1], None,
                                              ALU.mult)
                    i.then_inc(norm_done, 1)

                def out(h):
                    if not attend:
                        return
                    b = (p - 1) * 2 + h
                    at = (2 * (1 - par) + h) * S
                    dve.wait_ge(pv_mm, b + 1)
                    dve.tensor_tensor(ot[:, :, at:at + S], ps[:, OUT, 0:P].rearrange("p (g q) -> p g q", g=C),
                                      w["v_last"][:, b, :].unsqueeze(2).to_broadcast([P, C, S]),
                                      ALU.add).then_inc(o_done, 1)

                def quad_out():
                    k = p // 2 - 1 if isinstance(p, int) else loop[0]
                    dve.wait_ge(o_done, k * 4 + 4)
                    wait(dve, op_mm, k)
                    dve.tensor_copy(ot_hi[:], ot[:]).then_inc(ot_hi_done, 1)
                    dve.wait_ge(ot_hi_done, k + 1)
                    dve.tensor_tensor(ot_lo[:], ot[:], ot_hi[:].bitcast(F32), ALU.subtract).then_inc(ot_done, 1)
                    dve.wait_ge(x_in, k * 16 + 16)
                    dve.tensor_tensor(x[:], x[:], bo[:], ALU.add).then_inc(xb_done, 1)
                    dve.wait_ge(xb_done, k + 1)
                    wait(dve, x2_stored, k * 16)
                    dve.wait_ge(op_mm, k + 1)
                    dve.tensor_tensor(x2[:], ps[:, OUT, :], x[:], ALU.add).then_inc(x2_done, 1)

                mask_rows(0)
                if project:
                    dve.wait_ge(mask_in, p * 64 + 64)
                    dve.tensor_scalar(mask[:, par], mask_raw[:], 0.0, MASKED, ALU.is_equal,
                                      ALU.mult).then_inc(mask_ready, 1)
                if ahead:
                    split(p + 1, 1 - par, 0)
                norm(0)
                mask_rows(1)
                if ahead:
                    split(p + 1, 1 - par, 1)
                norm(1)
                out(0)
                out(1)
                if attend and par == 0:
                    quad_out()

            for par in range(2):
                for g in range(C):
                    for h in range(2):
                        i = dve.tensor_copy(kt[:, par, g, h, NK:KEYS], w["bk"][:, g:g + 1])
            i.then_inc(bk_ready, 1)
            dve.wait_ge(bo_in, 16)
            split(0, 0, 0)
            split(0, 0, 1)
            step(0, 0, attend=False)
            step(1, 1)
            step(2, 0)
            with dve.Fori(FIRST, LAST) as i:
                loop[0] = i
                step(i * 2 + 1, 1)
                step(i * 2 + 2, 0)
            step(PAIRS - 1, 1, ahead=False)
            step(PAIRS, 0, project=False, ahead=False)

        @block.tensor
        def _(pe):
            def step(p, par, attend=True, project=True, ahead=True):
                def project_block(n):
                    if not project:
                        return
                    if n == 0:
                        pe.wait_ge(cx_done, p * 2 + 2)
                    wait(pe, proj_evac, p * 8 + (n - 1))
                    out = ps[:, PROJ[n % 2], :]
                    if n < 4:
                        r = slice(n * P, (n + 1) * P)
                        i = product3(pe, out, lambda c: w["wk_hi"][:, c, r], lambda c: w["wk_lo"][:, c, r],
                                     lambda c: cx_hi[:, par, c, :], lambda c: cx_lo[:, par, c, :])
                    else:
                        r = slice((n - 4) * P, (n - 3) * P)
                        i = product3(pe, out, lambda c: cx_hi[:, par, c, r], lambda c: cx_lo[:, par, c, r],
                                     lambda c: w["wv_hi"][:, c, :], lambda c: w["wv_lo"][:, c, :])
                    i.then_inc(proj_mm, 1)

                def scores(h):
                    if not attend:
                        return
                    b = (p - 1) * 2 + h
                    pe.wait_ge(qb_ready, b * 4 + 4)
                    if h == 0:
                        pe.wait_ge(proj_evac, p * 8)
                    for g in range(C):
                        first = par == 0 and h == 0 and g == 0
                        wait(pe, masked, b * 4 if first else b * 4 + (g - 2))
                        pe.matmul(ps[:, bank(g, h, par), 0:KEYS], qb[:, h, g, :], kt[:, 1 - par, g, h, :],
                                  start=True, stop=True).then_inc(sc_mm, 1)

                def transposes(h):
                    if not attend:
                        return
                    b = (p - 1) * 2 + h
                    pe.wait_ge(norm_done, b + 1)
                    for kc in range(2):
                        wait(pe, pt_evac, b * 2 + (kc - 1))
                        for g in range(C):
                            i = pe.transpose(ps[:, PT[kc], g * P:(g + 1) * P], pr[:, h, g, kc * P:(kc + 1) * P],
                                             w["ident"][:])
                        i.then_inc(pt_mm, 1)

                def values(h):
                    if not attend:
                        return
                    b = (p - 1) * 2 + h
                    pe.wait_ge(pt_evac, b * 2 + 2)
                    wait(pe, o_done, b)
                    if par == 1 and h == 0:
                        wait(pe, x2_done, p // 2 if isinstance(p, int) else loop[0])
                    for g in range(C):
                        for kc in range(2):
                            for j in range(HG):
                                f = g * P + j * DK
                                i = pe.matmul(ps[j * DK:(j + 1) * DK, OUT, g * S:(g + 1) * S],
                                              v[:, 1 - par, 2 * h + kc, f:f + DK],
                                              pt[:, h, kc, f:f + DK], start=(kc == 0), stop=(kc == 1))
                    i.then_inc(pv_mm, 1)

                def out_projection():
                    k = p // 2 - 1 if isinstance(p, int) else loop[0]
                    pe.wait_ge(ot_done, k + 1)
                    product3(pe, ps[:, OUT, :], lambda c: ot_hi[:, c, :], lambda c: ot_lo[:, c, :],
                             lambda c: w["wo_hi"][:, c, :], lambda c: w["wo_lo"][:, c, :]).then_inc(op_mm, 1)

                project_block(0)
                scores(0)
                project_block(1)
                scores(1)
                project_block(2)
                transposes(0)
                project_block(3)
                values(0)
                transposes(1)
                project_block(4)
                values(1)
                project_block(5)
                project_block(6)
                if attend and par == 0:
                    out_projection()
                project_block(7)

            loop = [None]
            pe.wait_ge(bk_ready, 1)
            step(0, 0, attend=False)
            step(1, 1)
            step(2, 0)
            with pe.Fori(FIRST, LAST) as i:
                loop[0] = i
                step(i * 2 + 1, 1)
                step(i * 2 + 2, 0)
            step(PAIRS - 1, 1)
            step(PAIRS, 0, project=False)


def phase_c(nc, io, w, scr):
    with ExitStack() as ctx:
        def sb(name, shape, dt=F32):
            return ctx.enter_context(nc.sbuf_tensor("c_" + name, shape, dt))

        def sem(name):
            return ctx.enter_context(nc.semaphore("c_" + name))

        NW = 5
        w_hi = [sb(f"w_hi{k}", [P, C, D], F32R) for k in range(NW)]
        w_lo = [sb(f"w_lo{k}", [P, C, D], F32R) for k in range(NW)]
        xl = sb("xl", [P, TILES, D])
        res = sb("res", [P, TILES, D])
        xn3 = sb("xn3", [P, TILES, D])
        xt2_hi = sb("xt2_hi", [P, C, SUP], F32R)
        xt2_lo = sb("xt2_lo", [P, C, SUP], F32R)
        xt3_hi = sb("xt3_hi", [P, C, SUP], F32R)
        xt3_lo = sb("xt3_lo", [P, C, SUP], F32R)
        qb = sb("qb", [P, C, TILES, SUP])
        k = sb("k", [P, C, SUP])
        v = sb("v", [P, TILES, D])
        pr = sb("pr", [P, 4, SUP])
        rden = sb("rden", [P, SUP])
        ot = sb("ot", [P, C, P])
        causal = sb("causal", [P, P])
        ones = sb("ones", [P, DK])
        bf = sb("bf", [P, D])
        stats = sb("stats", [P, TILES, 6])
        mv = sb("mv", [P, TILES, 2])
        small = sb("small", [P, 4, TILES])
        gate = sb("gate", [1, 1])
        ps = ctx.enter_context(nc.psum_tensor("c_ps", [P, 8, 512], F32))
        PROJ, TRN, SC, OT, DEN = (0, 1), (2, 3), (4, 5), (6, 2), (7, 3)
        staging = (k, v, pr, res, xn3)

        w_in = [sem(f"w_in{n}") for n in range(NW)]
        w_hi_done, w_lo_done = sem("w_hi_done"), sem("w_lo_done")
        bf_in, xl_in, res_in, stored = sem("bf_in"), sem("xl_in"), sem("res_in"), sem("stored")
        consts = sem("consts")
        zeroed = sem("zeroed")
        var2, half2, seed2, step2, xn2_done = (sem(n) for n in ("var2", "half2", "seed2", "step2", "xn2_done"))
        var3, half3, seed3, step3, xn3_done = (sem(n) for n in ("var3", "half3", "seed3", "step3", "xn3_done"))
        t2_mm, t2_hi, t2_lo = sem("t2_mm"), sem("t2_hi"), sem("t2_lo")
        t3_mm, t3_hi, t3_lo = sem("t3_mm"), sem("t3_hi"), sem("t3_lo")
        qkv_mm, qkv_evac = sem("qkv_mm"), sem("qkv_evac")
        sc_mm, clipped, exp_done, pr_done, pv_mm = (
            sem(n) for n in ("sc_mm", "clipped", "exp_done", "pr_done", "pv_mm"))
        den_done, o_done, o_hi, o_lo = (sem(n) for n in ("den_done", "o_done", "o_hi", "o_lo"))
        out_mm, x3_done, xb_done, ffn_mm, y_done = (
            sem(n) for n in ("out_mm", "x3_done", "xb_done", "ffn_mm", "y_done"))
        block = ctx.enter_context(nc.Block())

        def steps(eng, step):
            step(0, prev=False)
            step(1)
            with eng.Fori(2, NSUP - 1) as s:
                step(s)
            step(NSUP - 1, more=False)

        @block.sync
        def _(sp):
            def load_xl(s):
                wait(sp, t2_mm, s * 4)
                sp.dma_start(xl[:], scr["x2_sup"][s]).then_inc(xl_in, 16)

            def load_res(s):
                wait(sp, stored, s * 16)
                sp.dma_start(res[:], scr["x2_sup"][s]).then_inc(res_in, 16)

            def store(s):
                sp.wait_ge(y_done, s * 4 + 4)
                sp.dma_start(io["out"][s], res[:]).then_inc(stored, 16)

            def step(s, prev=True, more=True):
                if more:
                    load_xl(s + 1)
                if prev:
                    store(s - 1)
                load_res(s)

            load_xl(0)
            for n in range(4):
                sp.dma_start(staging[n][:], io["wqkv"][n] if n < 3 else io["wout"]).then_inc(w_in[n], 16)
            chosen = sp.alloc_register("chosen")
            sp.reg_load(chosen, w["choice"][0:1, 0:1])
            choice = sp.snap(chosen, min_val=0, max_val=OPS - 1)
            sp.dma_start(xn3[:], io["W"][choice]).then_inc(w_in[4], 16)
            sp.dma_start(bf[:], io["b"][choice].partition_broadcast(P)).then_inc(bf_in, 16)
            sp.wait_ge(w_lo_done, 4)
            steps(sp, step)
            store(NSUP - 1)
            sp.wait_ge(stored, 16 * NSUP)

        @block.gpsimd
        def _(pool):
            pool.memset(causal[:], 1.0).then_inc(consts, 1)
            pool.memset(ones[:], 1.0).then_inc(consts, 1)
            pool.wait_ge(consts, 2)
            pool.affine_select(out=causal[:], in_=causal[:], compare_op=ALU.is_ge, fill=0.0, base=0,
                               pattern=[[1, P]], channel_multiplier=-1).then_inc(consts, 1)
            pool.wait_ge(consts, 3)
            blocks = causal[:].rearrange("p (b q) -> p b q", q=S)
            pool.affine_select(out=blocks, in_=blocks, compare_op=ALU.is_ge, fill=0.0, base=0,
                               pattern=[[-S, P // S], [0, S]], channel_multiplier=1).then_inc(consts, 1)
            pool.wait_ge(consts, 4)
            pool.wait_ge(bf_in, 16)

            def add_bias(s):
                pool.wait_ge(xn3_done, s + 1)
                pool.tensor_tensor(res[:], res[:], bf[:].unsqueeze(1).to_broadcast([P, TILES, D]),
                                   ALU.add).then_inc(xb_done, 1)

            def step(s, prev=True, more=True):
                if prev:
                    add_bias(s - 1)
                for n in range(16):
                    pool.wait_ge(exp_done, s * 16 + (n + 1))
                    m = pr[:, n % 4, :].rearrange("p (j q) -> p j q", j=HG)
                    pool.tensor_tensor(m, m, causal[:].unsqueeze(1).to_broadcast([P, HG, P]),
                                       ALU.mult).then_inc(pr_done, 1)

            steps(pool, step)
            add_bias(NSUP - 1)

        @block.scalar
        def _(act):
            def highs(s, mm, hi_sem, hi, free, count):
                for c in range(C):
                    act.wait_ge(mm, s * 4 + (c + 1))
                    if c == 0:
                        wait(act, free, count)
                    act.copy(hi[:, c, :], ps[:, TRN[c % 2], :]).then_inc(hi_sem, 1)

            def step(s, prev=True, more=True):
                def evac(n):
                    act.wait_ge(qkv_mm, s * 12 + (n + 1))
                    bank = ps[:, PROJ[n % 2], :]
                    if n < 4:
                        if n == 0:
                            wait(act, pv_mm, s * 16)
                        for j in range(HG):
                            r = slice(j * DK, (j + 1) * DK)
                            i = act.activation(qb[r, n, :, j * P:(j + 1) * P],
                                               bank[r].rearrange("p (t q) -> p t q", q=P), ACT.Copy, scale=SCALE)
                    elif n < 8:
                        i = act.copy(k[:, n - 4, :], bank)
                    else:
                        i = act.copy(v[:, n - 8, :], bank)
                    i.then_inc(qkv_evac, 1)

                def o_high(t):
                    act.wait_ge(o_done, s * 4 + (t + 1))
                    if t == 0:
                        wait(act, ffn_mm, s * 4)
                    act.copy(xt3_hi[:, :, t * P:(t + 1) * P], ot[:]).then_inc(o_hi, 1)

                evac(0)
                if prev:
                    rsqrt_seed(act, small, var3, half3, seed3, s - 1)
                evac(1)
                evac(2)
                if more:
                    rsqrt_seed(act, small, var2, half2, seed2, s + 1)
                for n in range(3, 12):
                    evac(n)
                if prev:
                    highs(s - 1, t3_mm, t3_hi, xt3_hi, out_mm, s * 4)
                for n in range(16):
                    act.wait_ge(clipped, s * 16 + (n + 1))
                    act.activation(pr[:, n % 4, :], pr[:, n % 4, :], ACT.Exp).then_inc(exp_done, 1)
                    if n % 4 == 2 and n > 4:
                        o_high(n // 4 - 1)
                o_high(3)
                if more:
                    highs(s + 1, t2_mm, t2_hi, xt2_hi, qkv_mm, s * 12 + 12)

            rsqrt_seed(act, small, var2, half2, seed2, 0)
            for n in range(3):
                act.wait_ge(w_in[n], 16)
                act.copy(w_hi[n][:].rearrange("p c n -> p (c n)"),
                         staging[n][:].rearrange("p a b -> p (a b)")).then_inc(w_hi_done, 1)
            highs(0, t2_mm, t2_hi, xt2_hi, None, 0)
            for n in range(3, NW):
                act.wait_ge(w_in[n], 16)
                act.copy(w_hi[n][:].rearrange("p c n -> p (c n)"),
                         staging[n][:].rearrange("p a b -> p (a b)")).then_inc(w_hi_done, 1)
            act.wait_ge(w_lo_done, 5)
            act.wait_ge(zeroed, 1)
            steps(act, step)
            rsqrt_seed(act, small, var3, half3, seed3, NSUP - 1)
            highs(NSUP - 1, t3_mm, t3_hi, xt3_hi, out_mm, NSUP * 4)

        @block.vector
        def _(dve):
            def ln2(s):
                dve.wait_ge(xl_in, s * 16 + 16)
                normalise(dve, xl, xl, stats, mv, small, gate[:], var2, seed2, xn2_done, step2,
                          s * LN_STEPS, s)

            def ln3(s):
                dve.wait_ge(x3_done, s * 4 + 4)
                wait(dve, t3_mm, s * 4)
                normalise(dve, res, xn3, stats, mv, small, gate[:], var3, seed3, xn3_done, step3,
                          s * LN_STEPS, s)

            def lows(s, hi_sem, lo_sem, hi, lo):
                for c in range(C):
                    dve.wait_ge(hi_sem, s * 4 + (c + 1))
                    dve.tensor_tensor(lo[:, c, :], ps[:, TRN[c % 2], :], hi[:, c, :].bitcast(F32),
                                      ALU.subtract).then_inc(lo_sem, 1)

            def ffn_add(s):
                dve.wait_ge(xb_done, s + 1)
                for t in range(TILES):
                    dve.wait_ge(ffn_mm, s * 4 + (t + 1))
                    dve.tensor_tensor(res[:, t, :], ps[:, PROJ[t % 2], :], res[:, t, :],
                                      ALU.add).then_inc(y_done, 1)

            def step(s, prev=True, more=True):
                def norm(t):
                    dve.wait_ge(pv_mm, s * 16 + (4 * t + 4))
                    dve.reciprocal(rden[:], ps[:, DEN[t % 2], :]).then_inc(den_done, 1)
                    dve.wait_ge(den_done, s * 4 + (t + 1))
                    dve.tensor_tensor(ot[:].rearrange("p c q -> p (c q)"), ps[:, OT[t % 2], :], rden[:],
                                      ALU.mult).then_inc(o_done, 1)

                def o_low(t):
                    dve.wait_ge(o_hi, s * 4 + (t + 1))
                    dve.tensor_tensor(xt3_lo[:, :, t * P:(t + 1) * P], ot[:],
                                      xt3_hi[:, :, t * P:(t + 1) * P].bitcast(F32), ALU.subtract).then_inc(o_lo, 1)

                if prev:
                    ln3(s - 1)
                if more:
                    ln2(s + 1)
                if prev:
                    lows(s - 1, t3_hi, t3_lo, xt3_hi, xt3_lo)
                    ffn_add(s - 1)
                for n in range(16):
                    dve.wait_ge(sc_mm, s * 16 + (n + 1))
                    wait(dve, pv_mm, s * 16 + (n - 3))
                    dve.tensor_scalar(pr[:, n % 4, :], ps[:, SC[n % 2], :], 10.0, -10.0, ALU.min,
                                      ALU.max).then_inc(clipped, 1)
                    if n > 4 and n % 4 == 2:
                        norm(n // 4 - 1)
                    if n > 4 and n % 4 == 3:
                        o_low(n // 4 - 1)
                norm(3)
                o_low(3)
                if more:
                    lows(s + 1, t2_hi, t2_lo, xt2_hi, xt2_lo)
                dve.wait_ge(res_in, s * 16 + 16)
                for t in range(TILES):
                    dve.wait_ge(out_mm, s * 4 + (t + 1))
                    dve.tensor_tensor(res[:, t, :], ps[:, PROJ[t % 2], :], res[:, t, :],
                                      ALU.add).then_inc(x3_done, 1)

            def split_low(n):
                dve.wait_ge(w_hi_done, n + 1)
                dve.tensor_tensor(w_lo[n][:].rearrange("p c n -> p (c n)"),
                                  staging[n][:].rearrange("p a b -> p (a b)"),
                                  w_hi[n][:].bitcast(F32).rearrange("p c n -> p (c n)"),
                                  ALU.subtract).then_inc(w_lo_done, 1)

            ln2(0)
            dve.memset(qb[:], 0.0).then_inc(zeroed, 1)
            for n in range(3):
                split_low(n)
            lows(0, t2_hi, t2_lo, xt2_hi, xt2_lo)
            for n in range(3, NW):
                split_low(n)
            steps(dve, step)
            ln3(NSUP - 1)
            lows(NSUP - 1, t3_hi, t3_lo, xt3_hi, xt3_lo)
            ffn_add(NSUP - 1)

        @block.tensor
        def _(pe):
            def transposes(s, x, ready, mm, lo_sem):
                pe.wait_ge(ready, s + 1)
                for c in range(C):
                    if c >= 2:
                        wait(pe, lo_sem, s * 4 + (c - 1))
                    for t in range(TILES):
                        i = pe.transpose(ps[:, TRN[c % 2], t * P:(t + 1) * P], x[:, t, c * P:(c + 1) * P],
                                         w["ident"][:])
                    i.then_inc(mm, 1)

            def tile_products(s, x_hi, x_lo, n, mm, done, before, count, ready=None):
                for t in range(TILES):
                    if ready is not None:
                        pe.wait_ge(ready, s * 4 + (t + 1))
                    if t < 2:
                        pe.wait_ge(before, count + (t - 1))
                    else:
                        pe.wait_ge(done, s * 4 + (t - 1))
                    r = slice(t * P, (t + 1) * P)
                    product3(pe, ps[:, PROJ[t % 2], :], lambda c: x_hi[:, c, r], lambda c: x_lo[:, c, r],
                             lambda c: w_hi[n][:, c, :], lambda c: w_lo[n][:, c, :]).then_inc(mm, 1)

            def ffn(s, before, count):
                transposes(s, xn3, xn3_done, t3_mm, t3_lo)
                pe.wait_ge(t3_lo, s * 4 + 4)
                tile_products(s, xt3_hi, xt3_lo, 4, ffn_mm, y_done, before, count)

            def step(s, prev=True, more=True):
                pe.wait_ge(t2_lo, s * 4 + 4)
                for n in range(12):
                    if n >= 2:
                        pe.wait_ge(qkv_evac, s * 12 + (n - 1))
                    else:
                        wait(pe, x3_done, s * 4 + (n - 1))
                    out = ps[:, PROJ[n % 2], :]
                    if n < 8:
                        r = slice((n % 4) * P, (n % 4 + 1) * P)
                        i = product3(pe, out, lambda c: w_hi[n // 4][:, c, r], lambda c: w_lo[n // 4][:, c, r],
                                     lambda c: xt2_hi[:, c, :], lambda c: xt2_lo[:, c, :])
                    else:
                        r = slice((n - 8) * P, (n - 7) * P)
                        i = product3(pe, out, lambda c: xt2_hi[:, c, r], lambda c: xt2_lo[:, c, r],
                                     lambda c: w_hi[2][:, c, :], lambda c: w_lo[2][:, c, :])
                    i.then_inc(qkv_mm, 1)
                if prev:
                    ffn(s - 1, qkv_evac, s * 12 + 12)

                def values(n):
                    t, g = n // 4, n % 4
                    pe.wait_ge(pr_done, s * 16 + (n + 1))
                    if g == 0:
                        wait(pe, o_done, s * 4 + (t - 1))
                    for j in range(HG):
                        r = slice(j * DK, (j + 1) * DK)
                        m = pr[:, g, j * P:(j + 1) * P]
                        pe.matmul(ps[r, OT[t % 2], g * P:(g + 1) * P],
                                  v[:, t, g * P + j * DK:g * P + (j + 1) * DK], m, start=True, stop=True)
                    for j in range(HG):
                        r = slice(j * DK, (j + 1) * DK)
                        m = pr[:, g, j * P:(j + 1) * P]
                        i = pe.matmul(ps[r, DEN[t % 2], g * P:(g + 1) * P], ones[:], m, start=True, stop=True)
                    i.then_inc(pv_mm, 1)

                pe.wait_ge(qkv_evac, s * 12 + 12)
                for n in range(16):
                    t, g = n // 4, n % 4
                    wait(pe, clipped, s * 16 + (n - 1))
                    pe.matmul(ps[:, SC[n % 2], :], k[:, g, t * P:(t + 1) * P], qb[:, g, t, :],
                              start=True, stop=True).then_inc(sc_mm, 1)
                    if n >= 2:
                        values(n - 2)
                values(14)
                values(15)
                pe.wait_ge(o_done, s * 4 + 4)
                if more:
                    transposes(s + 1, xl, xn2_done, t2_mm, t2_lo)
                if prev:
                    tile_products(s, xt3_hi, xt3_lo, 3, out_mm, x3_done, y_done, s * 4, ready=o_lo)
                else:
                    tile_products(s, xt3_hi, xt3_lo, 3, out_mm, x3_done, qkv_evac, s * 12 + 12, ready=o_lo)

            pe.wait_ge(consts, 4)
            transposes(0, xl, xn2_done, t2_mm, t2_lo)
            pe.wait_ge(w_lo_done, 5)
            steps(pe, step)
            ffn(NSUP - 1, x3_done, NSUP * 4)


def program(nc, io):
    scr_q = nc.dram_tensor("q_scratch", [PAIRS, P, C * 64], F32, kind="Internal").ap()
    scr_x2 = nc.dram_tensor("x2_scratch", [QUADS, P, D], F32, kind="Internal").ap()
    scr = {
        "q": scr_q.rearrange("(s a) p n -> s a p n", s=NSUP),
        "q_pairs": scr_q.rearrange("a p (g t) -> a p g t", g=C),
        "x2": scr_x2,
        "x2_sup": scr_x2.rearrange("(s t) p n -> s p t n", s=NSUP),
    }
    with ExitStack() as ctx:
        w = {
            "ident": ctx.enter_context(nc.sbuf_tensor("ident", [P, P], F32)),
            "choice": ctx.enter_context(nc.sbuf_tensor("choice", [1, OPS], U32)),
            "ident_ready": ctx.enter_context(nc.semaphore("ident_ready")),
        }
        with ExitStack() as cross:
            for name in ("wk", "wv", "wo"):
                for part in ("hi", "lo"):
                    w[f"{name}_{part}"] = cross.enter_context(
                        nc.sbuf_tensor(f"{name}_{part}", [P, C, D], F32R))
            w["v_last"] = cross.enter_context(nc.sbuf_tensor("v_last", [P, B, C], F32))
            w["bk"] = cross.enter_context(nc.sbuf_tensor("bk", [P, C], F32))
            phase_a(nc, io, w, scr)
            phase_b(nc, io, w, scr)
        phase_c(nc, io, w, scr)


def kernel(**inputs):
    import numpy as np
    import concourse.bacc as bacc
    from concourse.bass_utils import run_bass_kernel_spmd

    a = {n: np.asarray(v) for n, v in inputs.items()}
    ctx = a["ctx_1024"]
    arrays = {
        "x": a["x"].reshape(TOK, D),
        "ctx": ctx.reshape(B, KEYS, C, P).transpose(0, 3, 2, 1),
        "ctx_last": ctx[:, NK].reshape(B, C, P).transpose(2, 1, 0),
        "mask": a["mask_BxSxS2_ik0"].reshape(PAIRS, 2, S, KEYS).transpose(0, 2, 1, 3),
        "wqkv": a["L0_attn_Wqkv"].reshape(3, D, D).transpose(0, 2, 1),
        "wout": a["L0_attn_Wout"].T,
        "W": a["L0_ffn_W"], "b": a["L0_ffn_b"],
        "logits": a["L0_ffn_logits"].reshape(1, OPS), "u": a["L0_ffn_u"].reshape(1, OPS),
    }
    for n in ("Wq", "Wk", "Wv", "Wo"):
        arrays[n] = a["L0_xattn_" + n]
    for n in ("bq", "bk", "bv"):
        arrays[n] = a["L0_xattn_" + n].reshape(C, P).T
    arrays["bo"] = a["L0_xattn_bo"]
    arrays = {f"{n}_dram": np.ascontiguousarray(v) for n, v in arrays.items()}

    nc = bacc.Bacc("TRN2", target_bir_lowering=False, num_devices=1)
    t = {n[:-5]: nc.dram_tensor(n, v.shape, mybir.dt.from_np(v.dtype), kind="ExternalInput").ap()
         for n, v in arrays.items()}
    out = nc.dram_tensor("out_dram", (TOK, D), F32, kind="ExternalOutput").ap()
    io = dict(t)
    io["x"] = t["x"].rearrange("(s t p) n -> s t p n", s=NSUP, t=TILES)
    io["x_tiles"] = t["x"].rearrange("(k p) n -> k p n", p=P)
    io["out"] = out.rearrange("(s t p) n -> s p t n", s=NSUP, t=TILES)
    io["wqkv"] = t["wqkv"].rearrange("m (c p) n -> m p c n", p=P)
    io["W"] = t["W"].rearrange("m (c p) n -> m p c n", p=P)
    io["wout"] = t["wout"].rearrange("(c p) n -> p c n", p=P)
    for n in ("Wq", "Wk", "Wv", "Wo"):
        io[n] = t[n].rearrange("(c p) n -> p c n", p=P)
    program(nc, io)
    r = run_bass_kernel_spmd(nc, [arrays], core_ids=[0])
    return r.results[0]["out_dram"].reshape(B, S, D)
```

```python
import math
from contextlib import ExitStack

import concourse.bass as bass
from concourse import mybir

F32 = mybir.dt.float32
F32R = mybir.dt.float32r
I32 = mybir.dt.int32
U32 = mybir.dt.uint32
ALU = mybir.AluOpType
ACT = mybir.ActivationFunctionType
AX = mybir.AxisListType

P = 128
B, S, D, H = 128, 32, 512, 16
DK = D // H
KEYS = 257
NK = KEYS - 1
C = D // P
HG = P // DK
TOK = B * S
SUP = 512
NSUP = TOK // SUP
TILES = SUP // P
PAIRS = B // 2
QUADS = B // 4
OPS = 8
SCALE = float(DK) ** -0.5
EPS = 1e-5
MASKED = -1e30
FAR = 3.0e38


def wait(eng, sem, value):
    if not (isinstance(value, int) and value <= 0):
        eng.wait_ge(sem, value)


def product3(eng, out, w_hi, w_lo, m_hi, m_lo):
    last = None
    for c in range(C):
        for k, (w, m) in enumerate(((w_hi, m_hi), (w_hi, m_lo), (w_lo, m_hi))):
            last = eng.matmul(out, w(c), m(c), start=(c == 0 and k == 0), stop=(c == C - 1 and k == 2))
    return last


def inverse_deviation(dve, x, w, step_sem, base):
    stats, mv, small = w["stats"], w["mv"], w["small"]
    v, y, t2 = small[:, 0, :], small[:, 1, :], small[:, 2, :]
    for t in range(TILES):
        i = dve.bn_stats(stats[:, t, :], x[:, t, :])
    i.then_inc(step_sem, 1)
    dve.wait_ge(step_sem, base + 1)
    dve.memset(w["gate"][:], 0.0)
    for t in range(TILES):
        i = dve.bn_aggr(mv[:, t, :], stats[:, t, :])
    i.then_inc(step_sem, 1)
    dve.wait_ge(step_sem, base + 2)
    dve.tensor_scalar(v, mv[:, :, 1], EPS, None, ALU.add).then_inc(step_sem, 1)
    dve.wait_ge(step_sem, base + 3)
    dve.tensor_scalar(y.bitcast(I32), v.bitcast(I32), -0.5, MAGIC, ALU.mult, ALU.add).then_inc(step_sem, 1)
    for k in range(NEWTON):
        dve.wait_ge(step_sem, base + (4 + 3 * k))
        dve.scalar_tensor_tensor(t2, v, -0.5, y, ALU.mult, ALU.mult).then_inc(step_sem, 1)
        dve.wait_ge(step_sem, base + (5 + 3 * k))
        dve.tensor_tensor(t2, t2, y, ALU.mult).then_inc(step_sem, 1)
        dve.wait_ge(step_sem, base + (6 + 3 * k))
        dve.scalar_tensor_tensor(y, t2, 1.5, y, ALU.add, ALU.mult).then_inc(step_sem, 1)


def normalise(dve, x, xn, w, done, step_sem, base):
    dve.wait_ge(step_sem, base + LN_STEPS)
    for t in range(TILES):
        i = dve.tensor_scalar(xn[:, t, :], x[:, t, :], w["mv"][:, t, 0:1], w["small"][:, 1, t:t + 1],
                              ALU.subtract, ALU.mult)
    i.then_inc(done, 1)


def layer_norm(dve, x, xn, w, done, step_sem, base):
    inverse_deviation(dve, x, w, step_sem, base)
    normalise(dve, x, xn, w, done, step_sem, base)


MAGIC = 1597463007.0
NEWTON = 3
LN_STEPS = 4 + 3 * NEWTON


def split_context(dve, w, p, par, h):
    raw = w["ctx"][:, par, h]
    keys = slice(h * NK, (h + 1) * NK)
    for c in range(C):
        i = dve.tensor_scalar(w["split_hi"][:, par, c, keys], raw[:, c, 0:NK], raw[:, c, NK:KEYS],
                              None, ALU.subtract)
    i.then_inc(w["cx_hi_done"], 1)
    dve.wait_ge(w["cx_hi_done"], p * 2 + (h + 1))
    for c in range(C):
        i = dve.scalar_tensor_tensor(w["split_lo"][:, par, c, keys], raw[:, c, 0:NK], raw[:, c, NK:KEYS],
                                     w["split_hi"][:, par, c, keys].bitcast(F32), ALU.subtract, ALU.subtract)
    i.then_inc(w["cx_done"], 1)


def load_context(sp, io, w, p, par):
    for h in range(2):
        sp.dma_start(w["ctx"][:, par, h], io["ctx"][p * 2 + h]).then_inc(w["ctx_in"][par], 16)


def self_weight_high(act, w, n):
    act.wait_ge(w["w_in"][n], 16)
    act.copy(w["c_hi"][n].rearrange("p c n -> p (c n)"),
             w["staging"][n].rearrange("p c n -> p (c n)")).then_inc(w["w_hi_done"], 1)


def self_weight_low(dve, w, n):
    dve.wait_ge(w["w_hi_done"], n + 1)
    dve.tensor_tensor(w["c_lo"][n].rearrange("p c n -> p (c n)"), w["staging"][n].rearrange("p c n -> p (c n)"),
                      w["c_hi"][n].bitcast(F32).rearrange("p c n -> p (c n)"),
                      ALU.subtract).then_inc(w["w_lo_done"], 1)


def phase_a(nc, io, w, scr):
    with ExitStack() as ctx:
        def sb(name, shape, dt=F32):
            return ctx.enter_context(nc.sbuf_tensor("a_" + name, shape, dt))

        def sem(name):
            return ctx.enter_context(nc.semaphore("a_" + name))

        raw = sb("raw", [P, 4, C, D])
        wq_hi = sb("wq_hi", [P, C, D], F32R)
        wq_lo = sb("wq_lo", [P, C, D], F32R)
        last_t = sb("last_t", [P, C, B])
        bq = sb("bq", [P, C])
        bqs = sb("bqs", [P, C])
        bv = sb("bv", [P, C])
        x = sb("x", [P, 2, TILES, D])
        xt_hi, xt_lo = w["split_hi"], w["split_lo"]
        q = w["v"][:, 1].rearrange("p (a b) n -> p a (b n)", a=1).rearrange("p a (b g t) -> p (a b) g t", g=C, t=64)
        pick = sb("pick", [1, 8, OPS])
        best = sb("best", [1, OPS])
        ps = ctx.enter_context(nc.psum_tensor("a_ps", [P, 8, 512], F32))
        PROJ, TRN, VL = (0, 1), (2, 3), 4

        weights_in = [sem(f"weights_in{k}") for k in range(4)]
        consts_in, last_in, pick_in = sem("consts_in"), sem("last_in"), sem("pick_in")
        pick_act, pick_dve = sem("pick_act"), sem("pick_dve")
        x_in = [sem("x_in0"), sem("x_in1")]
        hi_done, lo_done = sem("hi_done"), sem("lo_done")
        bqs_done = sem("bqs_done")
        vl_mm, vl_done = sem("vl_mm"), sem("vl_done")
        step_sem, xn_done = sem("ln_step"), sem("xn_done")
        transposed = sem("transposed")
        xt_hi_done, xt_lo_done = sem("xt_hi_done"), sem("xt_lo_done")
        q_mm, q_evac = sem("q_mm"), sem("q_evac")
        q_stored = w["q_stored"]
        block = ctx.enter_context(nc.Block())
        hi = (wq_hi, w["wk_hi"], w["wv_hi"], w["wo_hi"])
        lo = (wq_lo, w["wk_lo"], w["wv_lo"], w["wo_lo"])

        @block.sync
        def _(sp):
            def load(s, par):
                wait(sp, transposed, 4 * (s - 1))
                sp.dma_start(x[:, par], io["x"][s].rearrange("t p n -> p t n")).then_inc(x_in[par], 16)

            def store(s):
                sp.wait_ge(q_evac, s * 4 + 4)
                sp.dma_start(scr["q"][s].rearrange("a p n -> p a n"),
                             q.rearrange("p a g t -> p a (g t)")).then_inc(q_stored, 16)

            load(0, 0)
            sp.dma_start(pick[:, 0, :], io["logits"]).then_inc(pick_in, 16)
            sp.dma_start(pick[:, 1, :], io["u"]).then_inc(pick_in, 16)
            names = ("Wq", "Wk", "Wv", "Wo")
            sp.dma_start(raw[:, 0], io["Wq"]).then_inc(weights_in[0], 16)
            sp.dma_start(bq[:], io["bq"]).then_inc(consts_in, 16)
            sp.dma_start(bv[:], io["bv"]).then_inc(consts_in, 16)
            sp.dma_start(w["bk"][:], io["bk"]).then_inc(consts_in, 16)
            load(1, 1)
            for k in (2, 1, 3):
                sp.dma_start(raw[:, k], io[names[k]]).then_inc(weights_in[k], 16)
            sp.dma_start(last_t[:], io["ctx_last"]).then_inc(last_in, 16)
            load(2, 0)
            load(3, 1)
            store(0)
            load(4, 0)
            store(1)
            with sp.Fori(1, NSUP // 2 - 2) as i:
                load(i * 2 + 3, 1)
                store(i * 2)
                load(i * 2 + 4, 0)
                store(i * 2 + 1)
            load(NSUP - 1, 1)
            store(NSUP - 4)
            load_context(sp, io, w, 0, 0)
            store(NSUP - 3)
            load_context(sp, io, w, 1, 1)
            store(NSUP - 2)
            store(NSUP - 1)
            sp.wait_ge(q_stored, 16 * (NSUP - 1))

        CHUNKS_AFTER = ((0, 1), (2, 3), (), ())

        def steps(eng, step, before_last):
            step(0, 0)
            step(1, 1)
            with eng.Fori(1, NSUP // 2 - 1) as i:
                step(i * 2, 0)
                step(i * 2 + 1, 1)
            step(NSUP - 2, 0, norm=False)
            before_last()
            step(NSUP - 1, 1, norm=False, turn=False)

        @block.scalar
        def _(act):
            def high(s, par, c):
                act.wait_ge(transposed, s * 4 + (c + 1))
                if c == 0:
                    wait(act, q_mm, (s - 1) * 4)
                act.copy(xt_hi[:, par, c, :], ps[:, TRN[c % 2], :]).then_inc(xt_hi_done, 1)

            def weight(k):
                act.wait_ge(weights_in[k], 16)
                act.copy(hi[k][:], raw[:, k]).then_inc(hi_done, 1)

            def step(s, par, norm=True, turn=True):
                if isinstance(s, int) and s < 2:
                    weight((2, 1)[s])
                for g in range(C):
                    act.wait_ge(q_mm, s * 4 + (g + 1))
                    if g == 0:
                        wait(act, q_stored, s * 16)
                    act.activation(q[:, :, g, :], ps[:, PROJ[g % 2], :].rearrange("p (a t) -> p a t", t=64),
                                   ACT.Identity, bias=bqs[:, g:g + 1], scale=SCALE).then_inc(q_evac, 1)
                    if turn:
                        for c in CHUNKS_AFTER[g]:
                            high(s + 1, 1 - par, c)

            def select():
                act.wait_ge(pick_in, 32)
                act.activation(pick[:, 6, :], pick[:, 1, :], ACT.Ln).then_inc(pick_act, 1)
                act.wait_ge(pick_act, 1)
                act.activation(pick[:, 1, :], pick[:, 6, :], ACT.Ln, scale=-1.0).then_inc(pick_act, 1)
                act.wait_ge(pick_dve, 2)
                act.activation(pick[:, 4, :], pick[:, 0, :], ACT.Exp, bias=pick[:, 3, 0:1],
                               accum_out=pick[:, 5, 0:1]).then_inc(pick_act, 1)
                act.wait_ge(pick_act, 3)
                act.activation(pick[:, 6, 0:1], pick[:, 5, 0:1], ACT.Ln).then_inc(pick_act, 1)

            select()
            weight(0)
            for c in range(C):
                high(0, 0, c)
            act.wait_ge(bqs_done, 1)
            steps(act, step, lambda: weight(3))

        @block.vector
        def _(dve):
            def ln_start(s, par, nth):
                dve.wait_ge(x_in[par], nth * 16)
                inverse_deviation(dve, x[:, par], w, step_sem, s * LN_STEPS)

            def ln_end(s, par):
                normalise(dve, x[:, par], x[:, par], w, xn_done, step_sem, s * LN_STEPS)

            def lows(s, par, chunks=range(C)):
                for c in chunks:
                    dve.wait_ge(xt_hi_done, s * 4 + (c + 1))
                    dve.tensor_tensor(xt_lo[:, par, c, :], ps[:, TRN[c % 2], :], xt_hi[:, par, c, :].bitcast(F32),
                                      ALU.subtract).then_inc(xt_lo_done, 1)

            def step(s, par, norm=True):
                if norm:
                    ln_start(s + 2, par, s // 2 + 2 if isinstance(s, int) else nth[0])
                lows(s + 1, 1 - par, (0, 1))
                if norm:
                    ln_end(s + 2, par)
                lows(s + 1, 1 - par, (2, 3))

            def last_values():
                dve.wait_ge(vl_mm, 1)
                for g in range(C):
                    i = dve.tensor_scalar(w["v_last"][:, :, g], ps[:, VL, g * B:(g + 1) * B], bv[:, g:g + 1],
                                          None, ALU.add)
                i.then_inc(vl_done, 1)

            def largest_logit():
                dve.wait_ge(pick_in, 32)
                dve.tensor_reduce(pick[:, 2, 0:1], pick[:, 0, :], AX.X, ALU.max).then_inc(pick_dve, 1)
                dve.wait_ge(pick_dve, 1)
                dve.tensor_scalar(pick[:, 3, 0:1], pick[:, 2, 0:1], -1.0, None, ALU.mult).then_inc(pick_dve, 1)

            def select():
                dve.wait_ge(pick_act, 4)
                dve.tensor_scalar(pick[:, 7, :], pick[:, 0, :], pick[:, 2, 0:1], pick[:, 6, 0:1], ALU.subtract,
                                  ALU.subtract).then_inc(pick_dve, 1)
                dve.wait_ge(pick_dve, 3)
                dve.tensor_tensor(pick[:, 4, :], pick[:, 7, :], pick[:, 1, :], ALU.subtract).then_inc(pick_dve, 1)
                dve.wait_ge(pick_dve, 4)
                dve.max(best[:], pick[:, 4, :]).then_inc(pick_dve, 1)
                dve.wait_ge(pick_dve, 5)
                dve.max_index(w["choice"][:], best[:], pick[:, 4, :]).then_inc(pick_dve, 1)

            nth = [None]
            largest_logit()
            ln_start(0, 0, 1)
            ln_end(0, 0)
            select()
            dve.wait_ge(consts_in, 48)
            dve.tensor_scalar(bqs[:], bq[:], SCALE, None, ALU.mult).then_inc(bqs_done, 1)
            lows(0, 0)
            ln_start(1, 1, 1)
            ln_end(1, 1)
            step(0, 0)
            step(1, 1)
            with dve.Fori(1, NSUP // 2 - 1) as i:
                nth[0] = i + 2
                step(i * 2, 0)
                step(i * 2 + 1, 1)
            step(NSUP - 2, 0, norm=False)
            last_values()
            dve.wait_ge(q_mm, (NSUP - 1) * 4)
            dve.wait_ge(w["ctx_in"][0], 32)
            split_context(dve, w, 0, 0, 0)
            split_context(dve, w, 0, 0, 1)

        @block.tensor
        def _(pe):
            def turn_chunk(s, par, c):
                if c == 0:
                    pe.wait_ge(xn_done, s + 1)
                wait(pe, xt_lo_done, s * 4 + (c - 1))
                for t in range(TILES):
                    i = pe.transpose(ps[:, TRN[c % 2], t * P:(t + 1) * P], x[:, par, t, c * P:(c + 1) * P],
                                     w["ident"][:])
                i.then_inc(transposed, 1)

            def step(s, par, norm=True, turn=True):
                pe.wait_ge(xt_lo_done, s * 4 + 4)
                for g in range(C):
                    wait(pe, q_evac, s * 4 + (g - 1))
                    product3(pe, ps[:, PROJ[g % 2], :],
                             lambda c: wq_hi[:, c, g * P:(g + 1) * P], lambda c: wq_lo[:, c, g * P:(g + 1) * P],
                             lambda c: xt_hi[:, par, c, :], lambda c: xt_lo[:, par, c, :]).then_inc(q_mm, 1)
                    if turn:
                        for c in CHUNKS_AFTER[g]:
                            turn_chunk(s + 1, 1 - par, c)

            def last_values():
                pe.wait_ge(weights_in[2], 16)
                pe.wait_ge(last_in, 16)
                for g in range(C):
                    for c in range(C):
                        i = pe.matmul(ps[:, VL, g * B:(g + 1) * B], raw[:, 2, c, g * P:(g + 1) * P],
                                      last_t[:, c, :], start=(c == 0), stop=(c == C - 1))
                i.then_inc(vl_mm, 1)

            pe.wait_ge(w["ident_ready"], 2)
            for c in range(C):
                turn_chunk(0, 0, c)
            pe.wait_ge(lo_done, 1)
            steps(pe, step, last_values)

        @block.gpsimd
        def _(pool):
            pool.memset(w["ident"][:], 0.0).then_inc(w["ident_ready"], 1)
            pool.wait_ge(w["ident_ready"], 1)
            pool.affine_select(out=w["ident"][:], in_=w["ident"][:], compare_op=ALU.not_equal, fill=1.0,
                               base=0, pattern=[[-1, P]], channel_multiplier=1).then_inc(w["ident_ready"], 1)
            for n, k in enumerate((0, 2, 1, 3)):
                pool.wait_ge(hi_done, n + 1)
                pool.tensor_tensor(lo[k][:], raw[:, k], hi[k][:].bitcast(F32), ALU.subtract).then_inc(lo_done, 1)


def phase_b(nc, io, w, scr):
    with ExitStack() as ctx:
        def sb(name, shape, dt=F32):
            return ctx.enter_context(nc.sbuf_tensor("b_" + name, shape, dt))

        def sem(name):
            return ctx.enter_context(nc.semaphore("b_" + name))

        cx_hi, cx_lo = w["split_hi"], w["split_lo"]
        kt_hi = sb("kt_hi", [P, 2, C, 2, KEYS + 1], F32R)
        kt_lo = sb("kt_lo", [P, 2, C, 2, KEYS + 1], F32R)
        v = w["v"]
        mask_raw = sb("mask_raw", [P, 2, KEYS], I32)
        mask = sb("mask", [P, 2, 2, KEYS])
        qt = sb("qt", [P, 2, C, 64])
        qb_hi = sb("qb_hi", [P, 2, C, P], F32R)
        qb_lo = sb("qb_lo", [P, 2, C, P], F32R)
        sm = sb("sm", [P, 2, C, KEYS])
        pr = sb("pr", [P, 2, C, KEYS])
        low = sb("low", [P, 2, C])
        rsum = sb("rsum", [P, 2, C])
        rinv = sb("rinv", [P, 2, C])
        pt = sb("pt", [P, 2, 2, D])
        ot = sb("ot", [P, C, P])
        ot_hi = sb("ot_hi", [P, C, P], F32R)
        ot_lo = sb("ot_lo", [P, C, P], F32R)
        x = sb("x", [P, D])
        x2 = w["row"]
        bo = sb("bo", [P, D])
        gate = sb("gates", [1, 2 * C])
        one = sb("one", [P, 1])
        ps = ctx.enter_context(nc.psum_tensor("b_ps", [P, 8, 512], F32))
        PROJ, SC, PT, OUT = (0, 1), (2, 3, 4), (5, 6), 7

        q_in = [sem("q_in0"), sem("q_in1")]
        mask_in, x_in, bo_in = sem("mask_in"), sem("x_in"), sem("bo_in")
        zeroed, bk_ready = sem("zeroed"), sem("bk_ready")
        qb_hi_done = sem("qb_hi_done")
        mask_ready, qb_ready = sem("mask_ready"), sem("qb_ready")
        ctx_in, cx_done = w["ctx_in"], w["cx_done"]
        proj_mm = sem("proj_mm")
        k_hi_done, k_done, v_done = sem("k_hi_done"), sem("k_done"), sem("v_done")
        sc_mm, masked, exp_done = sem("sc_mm"), sem("masked"), sem("exp_done")
        inv_done, norm_done = sem("inv_done"), sem("norm_done")
        pt_mm, pt_evac = sem("pt_mm"), sem("pt_evac")
        pv_mm, o_done = sem("pv_mm"), sem("o_done")
        ot_hi_done, ot_done = sem("ot_hi_done"), sem("ot_done")
        op_mm, xb_done, x2_done, x2_stored = sem("op_mm"), sem("xb_done"), sem("x2_done"), w["x2_stored"]
        block = ctx.enter_context(nc.Block())

        SCORES_AFTER = ((0, (0, 1)), (0, (2, 3)), (1, (0, 1)), (1, (2, 3)))

        def bank(g, h, par):
            return SC[(h * C + g + (2 if par else 0)) % 3]

        FIRST, LAST = 1, PAIRS // 2 - 1

        @block.sync
        def _(sp):
            def load_ctx(p, par):
                wait(sp, cx_done, (p - 1) * 2)
                load_context(sp, io, w, p, par)

            def load_small(p, par):
                wait(sp, mask_ready, p)
                for j in range(HG):
                    sp.dma_start(mask_raw[j * S:(j + 1) * S], io["mask"][p]).then_inc(mask_in, 16)
                wait(sp, qb_ready, (p - 1) * 8)
                sp.dma_start(qt[:, par], scr["q_pairs"][p]).then_inc(q_in[par], 16)

            def residual_in(k):
                wait(sp, x2_done, k)
                sp.dma_start(x[:], io["x_tiles"][k]).then_inc(x_in, 16)

            def result_out(k):
                sp.wait_ge(x2_done, k + 1)
                sp.dma_start(scr["x2"][k], x2[:]).then_inc(x2_stored, 16)

            def quad_io(k):
                residual_in(k)
                result_out(k)

            sp.dma_start(bo[:], io["bo"].partition_broadcast(P)).then_inc(bo_in, 16)
            load_small(0, 0)
            sp.wait_ge(w["q_stored"], 16 * NSUP)
            for p in range(3):
                load_ctx(p + 2, p % 2)
                load_small(p + 1, 1 - p % 2)
            quad_io(0)
            with sp.Fori(FIRST, LAST - 1) as i:
                load_ctx(i * 2 + 3, 1)
                load_small(i * 2 + 2, 0)
                load_ctx(i * 2 + 4, 0)
                load_small(i * 2 + 3, 1)
                quad_io(i)
            load_ctx(PAIRS - 1, 1)
            load_small(PAIRS - 2, 0)
            load_small(PAIRS - 1, 1)
            sp.wait_ge(cx_done, (PAIRS - 1) * 2)
            sp.wait_ge(x2_stored, 16 * TILES)
            sp.dma_start(w["xl"], scr["x2_sup"][0]).then_inc(w["xl_in"], 16)
            quad_io(QUADS - 2)
            residual_in(QUADS - 1)
            sp.wait_ge(cx_done, PAIRS * 2)
            sp.dma_start(w["staging"][0], io["wqkv"][0]).then_inc(w["w_in"][0], 16)
            sp.wait_ge(pv_mm, (PAIRS - 1) * 2)
            sp.dma_start(w["staging"][1], io["wqkv"][1]).then_inc(w["w_in"][1], 16)
            result_out(QUADS - 1)

        @block.gpsimd
        def _(pool):
            def expand(p, par, h, nth):
                if h == 0:
                    pool.wait_ge(q_in[par], nth * 16)
                wait(pool, sc_mm, (p * 2 + (h - 1)) * 4)
                for j in range(HG):
                    r = slice(j * DK, (j + 1) * DK)
                    pool.tensor_tensor(qb_hi[r, h, :, r], qt[r, par, :, h * S:(h + 1) * S],
                                       one[r].unsqueeze(1).to_broadcast([DK, C, S]), ALU.mult).then_inc(qb_hi_done, 1)
                for j in range(HG):
                    r = slice(j * DK, (j + 1) * DK)
                    pool.wait_ge(qb_hi_done, (p * 2 + h) * 4 + (j + 1))
                    pool.tensor_tensor(qb_lo[r, h, :, r], qt[r, par, :, h * S:(h + 1) * S],
                                       qb_hi[r, h, :, r].bitcast(F32), ALU.subtract).then_inc(qb_ready, 1)

            pool.memset(qb_hi[:].bitcast(F32), 0.0).then_inc(zeroed, 1)
            pool.memset(qb_lo[:].bitcast(F32), 0.0).then_inc(zeroed, 1)
            pool.memset(one[:], 1.0).then_inc(zeroed, 1)
            pool.wait_ge(zeroed, 3)
            for p in range(3):
                expand(p, p % 2, 0, p // 2 + 1)
                expand(p, p % 2, 1, p // 2 + 1)
            with pool.Fori(FIRST, LAST) as i:
                for n, par in ((1, 1), (2, 0)):
                    p = i * 2 + n
                    expand(p, par, 0, i + n)
                    expand(p, par, 1, i + n)
            p = PAIRS - 1
            expand(p, 1, 0, PAIRS // 2)
            expand(p, 1, 1, PAIRS // 2)

        @block.scalar
        def _(act):
            def step(p, par, attend=True, project=True, ahead=True):
                def evac(n):
                    if not project:
                        return
                    act.wait_ge(proj_mm, p * 8 + (n + 1))
                    if n < 4:
                        if n == 0:
                            wait(act, sc_mm, (p - 1) * 8)
                        act.activation(kt_hi[:, par, n, :, 0:NK], ps[:, PROJ[n % 2], :].rearrange(
                            "p (h k) -> p h k", h=2), ACT.Identity, bias=w["bk"][:, n:n + 1]).then_inc(k_hi_done, 1)
                    else:
                        if n == 4:
                            wait(act, pv_mm, (p - 1) * 2)
                            if isinstance(p, int) and p == 1:
                                act.wait_ge(w["q_stored"], 16 * NSUP)
                        act.copy(v[:, par, n - 4, :], ps[:, PROJ[n % 2], :]).then_inc(v_done, 1)

                def exps(h, groups):
                    if not attend:
                        return
                    b = (p - 1) * 2 + h
                    if groups[0] == 0:
                        wait(act, pt_mm, (b - 1) * 2)
                    for g in groups:
                        act.wait_ge(masked, b * 4 + (g + 1))
                        act.activation(pr[:, h, g, :], sm[:, h, g, :], ACT.Exp, bias=low[:, h, g:g + 1],
                                       scale=-1.0, accum_out=rsum[:, h, g:g + 1]).then_inc(exp_done, 1)

                def pt_out(h):
                    if not attend:
                        return
                    b = (p - 1) * 2 + h
                    for kc in range(2):
                        act.wait_ge(pt_mm, b * 2 + (kc + 1))
                        if kc == 0:
                            wait(act, pv_mm, b - 1)
                        act.copy(pt[:, h, kc, :], ps[:, PT[kc], :]).then_inc(pt_evac, 1)

                for n in range(4):
                    evac(n)
                    exps(*SCORES_AFTER[n])
                pt_out(0)
                evac(4)
                evac(5)
                pt_out(1)
                evac(6)
                evac(7)
                if not project:
                    act.wait_ge(proj_mm, PAIRS * 8)
                    self_weight_high(act, w, 0)
                    self_weight_high(act, w, 1)

            step(0, 0, attend=False)
            step(1, 1)
            step(2, 0)
            with act.Fori(FIRST, LAST) as i:
                step(i * 2 + 1, 1)
                step(i * 2 + 2, 0)
            step(PAIRS - 1, 1)
            step(PAIRS, 0, project=False)

        @block.vector
        def _(dve):
            def split(p, par, h):
                if h == 0:
                    wait(dve, proj_mm, (p - 1) * 8)
                    dve.wait_ge(ctx_in[par], in_count(p))
                split_context(dve, w, p, par, h)

            loop = [None]

            def in_count(p):
                return 32 * (p // 2 + 1) if isinstance(p, int) else loop[0] * 32 + 64

            def step(p, par, attend=True, project=True, ahead=True):
                def mask_rows(h, groups):
                    if not attend:
                        return
                    b = (p - 1) * 2 + h
                    if groups[0] == 0:
                        if h == 0:
                            dve.wait_ge(mask_ready, p)
                        wait(dve, exp_done, (b - 1) * 4)
                    for g in groups:
                        dve.wait_ge(sc_mm, b * 4 + (g + 1))
                        dve.memset(gate[:, h * C + g:h * C + g + 1], 0.0)
                        dve.tensor_tensor_reduce(sm[:, h, g, :], ps[:, bank(g, h, par), 0:KEYS],
                                                 mask[:, 1 - par, h, :], -1.0, FAR, ALU.add, ALU.min,
                                                 low[:, h, g:g + 1]).then_inc(masked, 1)

                def k_low(n):
                    if not project:
                        return
                    dve.wait_ge(k_hi_done, p * 4 + (n + 1))
                    dve.scalar_tensor_tensor(kt_lo[:, par, n, :, 0:NK], ps[:, PROJ[n % 2], :].rearrange(
                        "p (h k) -> p h k", h=2), w["bk"][:, n:n + 1], kt_hi[:, par, n, :, 0:NK].bitcast(F32),
                        ALU.add, ALU.subtract).then_inc(k_done, 1)

                def norm(h):
                    if not attend:
                        return
                    b = (p - 1) * 2 + h
                    dve.wait_ge(exp_done, b * 4 + 4)
                    dve.reciprocal(rinv[:, h, :], rsum[:, h, :]).then_inc(inv_done, 1)
                    dve.wait_ge(inv_done, b + 1)
                    for g in range(C):
                        i = dve.tensor_scalar(pr[:, h, g, 0:NK], pr[:, h, g, 0:NK], rinv[:, h, g:g + 1], None,
                                              ALU.mult)
                    i.then_inc(norm_done, 1)

                def out(h):
                    if not attend:
                        return
                    b = (p - 1) * 2 + h
                    at = (2 * (1 - par) + h) * S
                    dve.wait_ge(pv_mm, b + 1)
                    dve.tensor_tensor(ot[:, :, at:at + S], ps[:, OUT, 0:P].rearrange("p (g q) -> p g q", g=C),
                                      w["v_last"][:, b, :].unsqueeze(2).to_broadcast([P, C, S]),
                                      ALU.add).then_inc(o_done, 1)

                def quad_out():
                    k = p // 2 - 1 if isinstance(p, int) else loop[0]
                    dve.wait_ge(o_done, k * 4 + 4)
                    wait(dve, op_mm, k)
                    dve.tensor_copy(ot_hi[:], ot[:]).then_inc(ot_hi_done, 1)
                    dve.wait_ge(ot_hi_done, k + 1)
                    dve.tensor_tensor(ot_lo[:], ot[:], ot_hi[:].bitcast(F32), ALU.subtract).then_inc(ot_done, 1)
                    if not project:
                        self_weight_low(dve, w, 0)
                        self_weight_low(dve, w, 1)
                    dve.wait_ge(x_in, k * 16 + 16)
                    dve.tensor_tensor(x[:], x[:], bo[:], ALU.add).then_inc(xb_done, 1)
                    dve.wait_ge(xb_done, k + 1)
                    wait(dve, x2_stored, k * 16)
                    dve.wait_ge(op_mm, k + 1)
                    dve.tensor_tensor(x2[:], ps[:, OUT, :], x[:], ALU.add).then_inc(x2_done, 1)

                for n in range(4):
                    k_low(n)
                    mask_rows(*SCORES_AFTER[n])
                    if n == 0 and project:
                        dve.wait_ge(mask_in, p * 64 + 64)
                        dve.tensor_scalar(mask[:, par], mask_raw[:], 0.0, MASKED, ALU.is_equal,
                                          ALU.mult).then_inc(mask_ready, 1)
                    if n == 2:
                        norm(0)
                if ahead:
                    split(p + 1, 1 - par, 0)
                norm(1)
                out(0)
                if ahead:
                    split(p + 1, 1 - par, 1)
                elif project:
                    dve.wait_ge(w["xl_in"], 16)
                    layer_norm(dve, w["xl"], w["xl"], w, w["xn2_done"], w["ln2_step"], 0)
                out(1)
                if attend and par == 0:
                    quad_out()

            bk_cols = w["bk"][:].unsqueeze(2).unsqueeze(3).to_broadcast([P, C, 2, 2])
            for par in range(2):
                dve.tensor_copy(kt_hi[:, par, :, :, NK:], bk_cols).then_inc(bk_ready, 1)
            dve.wait_ge(bk_ready, 2)
            for par in range(2):
                dve.tensor_tensor(kt_lo[:, par, :, :, NK:], bk_cols, kt_hi[:, par, :, :, NK:].bitcast(F32),
                                  ALU.subtract).then_inc(bk_ready, 1)
            dve.wait_ge(bo_in, 16)
            step(0, 0, attend=False)
            step(1, 1)
            step(2, 0)
            with dve.Fori(FIRST, LAST) as i:
                loop[0] = i
                step(i * 2 + 1, 1)
                step(i * 2 + 2, 0)
            step(PAIRS - 1, 1, ahead=False)
            step(PAIRS, 0, project=False, ahead=False)

        @block.tensor
        def _(pe):
            def step(p, par, attend=True, project=True, ahead=True):
                def project_block(n):
                    if not project:
                        return
                    if n == 0:
                        pe.wait_ge(cx_done, p * 2 + 2)
                    if n < 2:
                        wait(pe, v_done, p * 4 + (n - 1))
                    elif n < 6:
                        pe.wait_ge(k_done, p * 4 + (n - 1))
                    else:
                        pe.wait_ge(v_done, p * 4 + (n - 5))
                    out = ps[:, PROJ[n % 2], :]
                    if n < 4:
                        r = slice(n * P, (n + 1) * P)
                        i = product3(pe, out, lambda c: w["wk_hi"][:, c, r], lambda c: w["wk_lo"][:, c, r],
                                     lambda c: cx_hi[:, par, c, :], lambda c: cx_lo[:, par, c, :])
                    else:
                        r = slice((n - 4) * P, (n - 3) * P)
                        i = product3(pe, out, lambda c: cx_hi[:, par, c, r], lambda c: cx_lo[:, par, c, r],
                                     lambda c: w["wv_hi"][:, c, :], lambda c: w["wv_lo"][:, c, :])
                    i.then_inc(proj_mm, 1)

                def scores(h, groups):
                    if not attend:
                        return
                    b = (p - 1) * 2 + h
                    if groups[0] == 0:
                        pe.wait_ge(qb_ready, b * 4 + 4)
                        if h == 0:
                            pe.wait_ge(k_done, p * 4)
                    for g in groups:
                        first = par == 0 and h == 0 and g == 0
                        wait(pe, masked, b * 4 if first else b * 4 + (g - 2))
                        out = ps[:, bank(g, h, par), 0:KEYS + 1]
                        k_hi, k_lo = kt_hi[:, 1 - par, g, h, :], kt_lo[:, 1 - par, g, h, :]
                        pe.matmul(out, qb_hi[:, h, g, :], k_hi, start=True, stop=False)
                        pe.matmul(out, qb_hi[:, h, g, :], k_lo, start=False, stop=False)
                        pe.matmul(out, qb_lo[:, h, g, :], k_hi, start=False, stop=True).then_inc(sc_mm, 1)

                def transposes(h):
                    if not attend:
                        return
                    b = (p - 1) * 2 + h
                    pe.wait_ge(norm_done, b + 1)
                    for kc in range(2):
                        wait(pe, pt_evac, b * 2 + (kc - 1))
                        for g in range(C):
                            i = pe.transpose(ps[:, PT[kc], g * P:(g + 1) * P], pr[:, h, g, kc * P:(kc + 1) * P],
                                             w["ident"][:])
                        i.then_inc(pt_mm, 1)

                def values(h):
                    if not attend:
                        return
                    b = (p - 1) * 2 + h
                    pe.wait_ge(pt_evac, b * 2 + 2)
                    pe.wait_ge(v_done, p * 4)
                    wait(pe, o_done, b)
                    if par == 1 and h == 0:
                        wait(pe, x2_done, p // 2 if isinstance(p, int) else loop[0])
                    for g in range(C):
                        for kc in range(2):
                            for j in range(HG):
                                f = g * P + j * DK
                                i = pe.matmul(ps[j * DK:(j + 1) * DK, OUT, g * S:(g + 1) * S],
                                              v[:, 1 - par, 2 * h + kc, f:f + DK],
                                              pt[:, h, kc, f:f + DK], start=(kc == 0), stop=(kc == 1))
                    i.then_inc(pv_mm, 1)

                def out_projection():
                    k = p // 2 - 1 if isinstance(p, int) else loop[0]
                    pe.wait_ge(ot_done, k + 1)
                    product3(pe, ps[:, OUT, :], lambda c: ot_hi[:, c, :], lambda c: ot_lo[:, c, :],
                             lambda c: w["wo_hi"][:, c, :], lambda c: w["wo_lo"][:, c, :]).then_inc(op_mm, 1)

                for n in range(4):
                    project_block(n)
                    scores(*SCORES_AFTER[n])
                transposes(0)
                project_block(4)
                values(0)
                project_block(5)
                transposes(1)
                project_block(6)
                values(1)
                project_block(7)
                if attend and par == 0:
                    out_projection()

            loop = [None]
            step(0, 0, attend=False)
            pe.wait_ge(bk_ready, 4)
            step(1, 1)
            step(2, 0)
            with pe.Fori(FIRST, LAST) as i:
                loop[0] = i
                step(i * 2 + 1, 1)
                step(i * 2 + 2, 0)
            step(PAIRS - 1, 1)
            step(PAIRS, 0, project=False)


def phase_c(nc, io, w, scr):
    with ExitStack() as ctx:
        def sb(name, shape, dt=F32):
            return ctx.enter_context(nc.sbuf_tensor("c_" + name, shape, dt))

        def sem(name):
            return ctx.enter_context(nc.semaphore("c_" + name))

        w_hi = [w["c_hi"][0], w["c_hi"][1], sb("wv_hi", [P, C, D], F32R)[:], sb("wout_hi", [P, C, D], F32R)[:],
                w["wo_hi"][:]]
        w_lo = [w["c_lo"][0], w["c_lo"][1], sb("wv_lo", [P, C, D], F32R)[:], sb("wout_lo", [P, C, D], F32R)[:],
                w["wo_lo"][:]]
        xl, res = w["xl"], w["res"]
        xn3 = sb("xn3", [P, TILES, D])
        (xt2_hi, xt2_lo), (xt3_hi, xt3_lo) = ((w["split_hi"][:, k], w["split_lo"][:, k]) for k in range(2))
        qb = sb("qb", [P, C, TILES, SUP])
        k, v = w["v"][:, 0], w["v"][:, 1]
        pr = sb("pr", [P, 4, SUP])
        rden = sb("rden", [P, 2, SUP])
        ot = sb("ot", [P, 2, C, P])
        E_LOW, E_HIGH = math.exp(-10.0), math.exp(10.0)
        causal = sb("causal", [P, P])
        ones = sb("ones", [P, DK])
        bf = w["row"]
        ps = ctx.enter_context(nc.psum_tensor("c_ps", [P, 8, 512], F32))
        PROJ, TRN, SC, OT, DEN = (0, 1), (2, 3), (4, 5), (6, 2), (7, 3)
        w = dict(w, c_hi=w_hi, c_lo=w_lo, staging=w["staging"] + (v, pr[:], xn3[:]))

        w_in, w_lo_done = w["w_in"], w["w_lo_done"]
        bf_in, xl_in, res_in, stored = sem("bf_in"), w["xl_in"], sem("res_in"), sem("stored")
        consts = sem("consts")
        zeroed = sem("zeroed")
        step2, xn2_done = w["ln2_step"], w["xn2_done"]
        step3, xn3_done = sem("ln3_step"), sem("xn3_done")
        t2_mm, t2_hi, t2_lo = sem("t2_mm"), sem("t2_hi"), sem("t2_lo")
        t3_mm, t3_hi, t3_lo = sem("t3_mm"), sem("t3_hi"), sem("t3_lo")
        qkv_mm, qkv_evac = sem("qkv_mm"), sem("qkv_evac")
        sc_mm, exp_done, pr_done, pv_mm, den_done = (
            sem(n) for n in ("sc_mm", "exp_done", "pr_done", "pv_mm", "den_done"))
        o_raw, o_done, o_hi, o_lo = (sem(n) for n in ("o_raw", "o_done", "o_hi", "o_lo"))
        out_mm, x3_done, xb_done, ffn_mm, y_done = (
            sem(n) for n in ("out_mm", "x3_done", "xb_done", "ffn_mm", "y_done"))
        block = ctx.enter_context(nc.Block())

        TURN3 = 7
        LAG = 3
        def steps(eng, step):
            step(0, prev=False)
            step(1)
            with eng.Fori(2, NSUP - 1) as s:
                step(s)
            step(NSUP - 1, more=False)

        @block.sync
        def _(sp):
            def load_xl(s):
                wait(sp, t2_mm, s * 4)
                sp.dma_start(xl, scr["x2_sup"][s]).then_inc(xl_in, 16)

            def load_res(s):
                wait(sp, stored, s * 16)
                sp.dma_start(res, scr["x2_sup"][s]).then_inc(res_in, 16)

            def store(s):
                sp.wait_ge(y_done, s * 4 + 4)
                sp.dma_start(io["out"][s], res).then_inc(stored, 16)

            def step(s, prev=True, more=True):
                if more:
                    load_xl(s + 1)
                if prev:
                    store(s - 1)
                load_res(s)

            sp.dma_start(w["staging"][2], io["wqkv"][2]).then_inc(w_in[2], 16)
            sp.dma_start(w["staging"][3], io["wout"]).then_inc(w_in[3], 16)
            chosen = sp.alloc_register("chosen")
            sp.reg_load(chosen, w["choice"][0:1, 0:1])
            choice = sp.snap(chosen, min_val=0, max_val=OPS - 1)
            sp.dma_start(xn3[:], io["W"][choice]).then_inc(w_in[4], 16)
            sp.wait_ge(w["x2_stored"], 16 * QUADS)
            sp.dma_start(bf[:], io["b"][choice].partition_broadcast(P)).then_inc(bf_in, 16)
            steps(sp, step)
            store(NSUP - 1)
            sp.wait_ge(stored, 16 * NSUP)

        @block.gpsimd
        def _(pool):
            for g in range(C):
                pool.memset(qb[:, g], 0.0).then_inc(zeroed, 1)
            pool.memset(causal[:], E_HIGH).then_inc(consts, 1)
            pool.memset(ones[:], 1.0).then_inc(consts, 1)
            pool.wait_ge(consts, 2)
            pool.affine_select(out=causal[:], in_=causal[:], compare_op=ALU.is_ge, fill=0.0, base=0,
                               pattern=[[1, P]], channel_multiplier=-1).then_inc(consts, 1)
            pool.wait_ge(consts, 3)
            blocks = causal[:].rearrange("p (b q) -> p b q", q=S)
            pool.affine_select(out=blocks, in_=blocks, compare_op=ALU.is_ge, fill=0.0, base=0,
                               pattern=[[-S, P // S], [0, S]], channel_multiplier=1).then_inc(consts, 1)
            pool.wait_ge(consts, 4)
            pool.wait_ge(bf_in, 16)

            def add_bias(s):
                pool.wait_ge(xn3_done, s + 1)
                pool.tensor_tensor(res, res, bf[:].unsqueeze(1).to_broadcast([P, TILES, D]),
                                   ALU.add).then_inc(xb_done, 1)

            def step(s, prev=True, more=True):
                if prev:
                    add_bias(s - 1)
                def o_low(t):
                    pool.wait_ge(o_hi, s * 4 + (t + 1))
                    pool.tensor_tensor(xt3_lo[:, :, t * P:(t + 1) * P], ot[:, t % 2],
                                       xt3_hi[:, :, t * P:(t + 1) * P].bitcast(F32), ALU.subtract).then_inc(o_lo, 1)

                for t in range(TILES):
                    pool.wait_ge(den_done, s * 16 + (4 * t + 4))
                    pool.wait_ge(o_raw, s * 4 + (t + 1))
                    o = ot[:, t % 2].rearrange("p c q -> p (c q)")
                    pool.tensor_tensor(o, o, rden[:, t % 2],
                                       ALU.mult).then_inc(o_done, 1)
                    o_low(t)

            steps(pool, step)
            add_bias(NSUP - 1)

        @block.scalar
        def _(act):
            def high(s, c, mm, hi_sem, hi, free, count):
                act.wait_ge(mm, s * 4 + (c + 1))
                if c == 0:
                    wait(act, free, count)
                act.copy(hi[:, c, :], ps[:, TRN[c % 2], :]).then_inc(hi_sem, 1)

            def step(s, prev=True, more=True):
                def evac(n):
                    act.wait_ge(qkv_mm, s * 12 + (n + 1))
                    bank = ps[:, PROJ[n % 2], :]
                    if n < 4:
                        if n == 0:
                            wait(act, pv_mm, s * 16)
                        if not prev:
                            act.wait_ge(zeroed, n + 1)
                        for j in range(HG):
                            r = slice(j * DK, (j + 1) * DK)
                            i = act.activation(qb[r, n, :, j * P:(j + 1) * P],
                                               bank[r].rearrange("p (t q) -> p t q", q=P), ACT.Copy, scale=SCALE)
                    elif n < 8:
                        i = act.copy(k[:, n - 4, :], bank)
                    else:
                        i = act.copy(v[:, n - 8, :], bank)
                    i.then_inc(qkv_evac, 1)

                def o_out(t):
                    act.wait_ge(pv_mm, s * 16 + (4 * t + 4))
                    wait(act, o_lo, s * 4 + (t - 1))
                    act.copy(ot[:, t % 2].rearrange("p c q -> p (c q)"), ps[:, OT[t % 2], :]).then_inc(o_raw, 1)

                def o_high(t):
                    act.wait_ge(o_done, s * 4 + (t + 1))
                    if t == 0:
                        wait(act, ffn_mm, s * 4)
                    act.copy(xt3_hi[:, :, t * P:(t + 1) * P], ot[:, t % 2]).then_inc(o_hi, 1)

                for n in range(12):
                    evac(n)
                    if prev and 0 <= n - TURN3 < C:
                        high(s - 1, n - TURN3, t3_mm, t3_hi, xt3_hi, out_mm, s * 4)
                    if not prev and n in (3, 7):
                        self_weight_high(act, w, 3 + (n == 7))
                if more:
                    for c in range(C):
                        high(s + 1, c, t2_mm, t2_hi, xt2_hi, qkv_mm, s * 12 + 12)
                if not prev:
                    act.wait_ge(w_lo_done, 4)
                for n in range(16):
                    act.wait_ge(sc_mm, s * 16 + (n + 1))
                    wait(act, pv_mm, s * 16 + (n - 3))
                    act.activation(pr[:, n % 4, :], ps[:, SC[n % 2], :], ACT.Exp).then_inc(exp_done, 1)
                    if n == 12:
                        o_high(0)
                    if n % 4 == 3 and n > 4:
                        o_out(n // 4 - 1)
                o_high(1)
                o_high(2)
                o_out(3)
                o_high(3)

            for c in range(C):
                high(0, c, t2_mm, t2_hi, xt2_hi, None, 0)
            self_weight_high(act, w, 2)
            steps(act, step)
            for c in range(C):
                high(NSUP - 1, c, t3_mm, t3_hi, xt3_hi, out_mm, NSUP * 4)

        @block.vector
        def _(dve):
            def ln2(s):
                dve.wait_ge(xl_in, s * 16 + 16)
                layer_norm(dve, xl, xl, w, xn2_done, step2, s * LN_STEPS)

            def ln3(s):
                dve.wait_ge(x3_done, s * 4 + 4)
                wait(dve, t3_mm, s * 4)
                layer_norm(dve, res, xn3, w, xn3_done, step3, s * LN_STEPS)

            def low(s, c, hi_sem, lo_sem, hi, lo):
                dve.wait_ge(hi_sem, s * 4 + (c + 1))
                dve.tensor_tensor(lo[:, c, :], ps[:, TRN[c % 2], :], hi[:, c, :].bitcast(F32),
                                  ALU.subtract).then_inc(lo_sem, 1)

            def ffn_add(s, t):
                if t == 0:
                    dve.wait_ge(xb_done, s + 1)
                dve.wait_ge(ffn_mm, s * 4 + (t + 1))
                dve.tensor_tensor(res[:, t, :], ps[:, PROJ[t % 2], :], res[:, t, :], ALU.add).then_inc(y_done, 1)

            def step(s, prev=True, more=True):
                def divide(n):
                    t, g = n // 4, n % 4
                    if g == 0:
                        dve.wait_ge(pv_mm, s * 16 + (n + C))
                        wait(dve, o_done, s * 4 + (t - 1))
                    dve.reciprocal(rden[:, t % 2, g * P:(g + 1) * P],
                                   ps[:, DEN[t % 2], g * P:(g + 1) * P]).then_inc(den_done, 1)
                def mask(n):
                    dve.wait_ge(exp_done, s * 16 + (n + 1))
                    m = pr[:, n % 4, :].rearrange("p (j q) -> p j q", j=HG)
                    dve.scalar_tensor_tensor(m, m, E_LOW, causal[:].unsqueeze(1).to_broadcast([P, HG, P]),
                                             ALU.max, ALU.min).then_inc(pr_done, 1)

                if prev:
                    ln3(s - 1)
                if more:
                    ln2(s + 1)
                if not prev:
                    self_weight_low(dve, w, 3)
                    self_weight_low(dve, w, 4)
                if prev:
                    for c in range(C):
                        low(s - 1, c, t3_hi, t3_lo, xt3_hi, xt3_lo)
                for t in range(TILES):
                    if prev:
                        ffn_add(s - 1, t)
                    if more:
                        low(s + 1, t, t2_hi, t2_lo, xt2_hi, xt2_lo)
                if not prev:
                    dve.wait_ge(consts, 4)
                for n in range(16):
                    mask(n)
                    if n >= LAG + C - 1:
                        divide(n - LAG - C + 1)
                for n in range(17 - LAG - C, 16):
                    divide(n)
                dve.wait_ge(res_in, s * 16 + 16)
                for t in range(TILES):
                    dve.wait_ge(out_mm, s * 4 + (t + 1))
                    dve.tensor_tensor(res[:, t, :], ps[:, PROJ[t % 2], :], res[:, t, :],
                                      ALU.add).then_inc(x3_done, 1)

            for c in range(C):
                low(0, c, t2_hi, t2_lo, xt2_hi, xt2_lo)
            self_weight_low(dve, w, 2)
            steps(dve, step)
            ln3(NSUP - 1)
            for c in range(C):
                low(NSUP - 1, c, t3_hi, t3_lo, xt3_hi, xt3_lo)
            for t in range(TILES):
                ffn_add(NSUP - 1, t)

        @block.tensor
        def _(pe):
            def turn_chunk(s, c, x, ready, mm, lo_sem):
                if c == 0:
                    pe.wait_ge(ready, s + 1)
                if c >= 2:
                    wait(pe, lo_sem, s * 4 + (c - 1))
                for t in range(TILES):
                    i = pe.transpose(ps[:, TRN[c % 2], t * P:(t + 1) * P], x[:, t, c * P:(c + 1) * P],
                                     w["ident"][:])
                i.then_inc(mm, 1)

            def tile_product(s, t, x_hi, x_lo, n, mm, done, before, count):
                if t < 2:
                    pe.wait_ge(before, count + (t - 1))
                else:
                    pe.wait_ge(done, s * 4 + (t - 1))
                r = slice(t * P, (t + 1) * P)
                product3(pe, ps[:, PROJ[t % 2], :], lambda c: x_hi[:, c, r], lambda c: x_lo[:, c, r],
                         lambda c: w_hi[n][:, c, :], lambda c: w_lo[n][:, c, :]).then_inc(mm, 1)

            def step(s, prev=True, more=True):
                pe.wait_ge(t2_lo, s * 4 + 4)
                for n in range(12):
                    if not prev and n in (0, 8):
                        pe.wait_ge(w_lo_done, 2 + n // 8)
                    if n >= 2:
                        pe.wait_ge(qkv_evac, s * 12 + (n - 1))
                    else:
                        wait(pe, x3_done, s * 4 + (n - 1))
                    out = ps[:, PROJ[n % 2], :]
                    if n < 8:
                        r = slice((n % 4) * P, (n % 4 + 1) * P)
                        i = product3(pe, out, lambda c: w_hi[n // 4][:, c, r], lambda c: w_lo[n // 4][:, c, r],
                                     lambda c: xt2_hi[:, c, :], lambda c: xt2_lo[:, c, :])
                    else:
                        r = slice((n - 8) * P, (n - 7) * P)
                        i = product3(pe, out, lambda c: xt2_hi[:, c, r], lambda c: xt2_lo[:, c, r],
                                     lambda c: w_hi[2][:, c, :], lambda c: w_lo[2][:, c, :])
                    i.then_inc(qkv_mm, 1)
                    if prev and 0 <= n - TURN3 < C:
                        turn_chunk(s - 1, n - TURN3, xn3, xn3_done, t3_mm, t3_lo)
                if prev:
                    pe.wait_ge(t3_lo, s * 4)
                for t in range(TILES):
                    if prev:
                        tile_product(s - 1, t, xt3_hi, xt3_lo, 4, ffn_mm, y_done, qkv_evac, s * 12 + 12)
                    if more:
                        turn_chunk(s + 1, t, xl, xn2_done, t2_mm, t2_lo)

                def values(n):
                    t, g = n // 4, n % 4
                    pe.wait_ge(pr_done, s * 16 + (n + 1))
                    if g == 0:
                        wait(pe, o_raw, s * 4 + (t - 1))
                        wait(pe, den_done, s * 16 + (4 * t - 4))
                        if t == 1 and more:
                            pe.wait_ge(t2_lo, s * 4 + 8)
                    for j in range(HG):
                        r = slice(j * DK, (j + 1) * DK)
                        m = pr[:, g, j * P:(j + 1) * P]
                        pe.matmul(ps[r, OT[t % 2], g * P:(g + 1) * P],
                                  v[:, t, g * P + j * DK:g * P + (j + 1) * DK], m, start=True, stop=True)
                    for j in range(HG):
                        r = slice(j * DK, (j + 1) * DK)
                        m = pr[:, g, j * P:(j + 1) * P]
                        i = pe.matmul(ps[r, DEN[t % 2], g * P:(g + 1) * P], ones[:], m, start=True, stop=True)
                    i.then_inc(pv_mm, 1)

                pe.wait_ge(qkv_evac, s * 12 + 12)
                if not prev:
                    pe.wait_ge(consts, 4)
                for n in range(16):
                    t, g = n // 4, n % 4
                    wait(pe, exp_done, s * 16 + (n - 1))
                    pe.matmul(ps[:, SC[n % 2], :], k[:, g, t * P:(t + 1) * P], qb[:, g, t, :],
                              start=True, stop=True).then_inc(sc_mm, 1)
                    if n >= LAG:
                        values(n - LAG)
                for n in range(16 - LAG, 16):
                    values(n)
                if not prev:
                    pe.wait_ge(w_lo_done, 5)
                for t in range(TILES):
                    pe.wait_ge(o_lo, s * 4 + (t + 1))
                    if prev:
                        tile_product(s, t, xt3_hi, xt3_lo, 3, out_mm, x3_done, y_done, s * 4)
                    else:
                        tile_product(s, t, xt3_hi, xt3_lo, 3, out_mm, x3_done, qkv_evac, s * 12 + 12)

            for c in range(C):
                turn_chunk(0, c, xl, xn2_done, t2_mm, t2_lo)
            steps(pe, step)
            for c in range(C):
                turn_chunk(NSUP - 1, c, xn3, xn3_done, t3_mm, t3_lo)
            pe.wait_ge(t3_lo, NSUP * 4)
            for t in range(TILES):
                tile_product(NSUP - 1, t, xt3_hi, xt3_lo, 4, ffn_mm, y_done, x3_done, NSUP * 4)


def program(nc, io):
    scr_q = nc.dram_tensor("q_scratch", [PAIRS, P, C * 64], F32, kind="Internal").ap()
    scr_x2 = nc.dram_tensor("x2_scratch", [QUADS, P, D], F32, kind="Internal").ap()
    scr = {
        "q": scr_q.rearrange("(s a) p n -> s a p n", s=NSUP),
        "q_pairs": scr_q.rearrange("a p (g t) -> a p g t", g=C),
        "x2": scr_x2,
        "x2_sup": scr_x2.rearrange("(s t) p n -> s p t n", s=NSUP),
    }
    with ExitStack() as ctx:
        def sb(name, shape, dt=F32):
            return ctx.enter_context(nc.sbuf_tensor(name, shape, dt))

        def sem(name):
            return ctx.enter_context(nc.semaphore(name))

        w = {"ident": sb("ident", [P, P]), "choice": sb("choice", [1, OPS], U32),
             "split_hi": sb("split_hi", [P, 2, C, SUP], F32R), "split_lo": sb("split_lo", [P, 2, C, SUP], F32R),
             "stats": sb("stats", [P, TILES, 6]), "mv": sb("mv", [P, TILES, 2]),
             "small": sb("small", [P, 3, TILES]), "gate": sb("gate", [1, 1])}
        for name in ("wk", "wv", "wo"):
            for part in ("hi", "lo"):
                w[f"{name}_{part}"] = sb(f"{name}_{part}", [P, C, D], F32R)
        raw = sb("raw", [P, 2, 2 * C * KEYS])
        w["ctx"] = raw[:].rearrange("p a (h c k) -> p a h c k", h=2, c=C)
        w["xl"], w["res"] = (raw[:, k, 0:TILES * D].rearrange("p (t n) -> p t n", n=D) for k in range(2))
        w["c_hi"], w["c_lo"] = ((w[f"wk_{part}"][:], w[f"wv_{part}"][:]) for part in ("hi", "lo"))
        w["v"] = sb("v", [P, 2, 4, D])
        w["row"] = sb("row", [P, D])
        w["staging"] = (w["res"], w["v"][:, 0])
        for name in ("ident_ready", "cx_hi_done", "cx_done", "xl_in", "xn2_done", "ln2_step", "w_hi_done",
                     "w_lo_done", "q_stored", "x2_stored"):
            w[name] = sem(name)
        w["ctx_in"] = [sem("ctx_in0"), sem("ctx_in1")]
        w["w_in"] = [sem(f"w_in{n}") for n in range(5)]
        with ExitStack() as cross:
            w["v_last"] = cross.enter_context(nc.sbuf_tensor("v_last", [P, B, C], F32))
            w["bk"] = cross.enter_context(nc.sbuf_tensor("bk", [P, C], F32))
            phase_a(nc, io, w, scr)
            phase_b(nc, io, w, scr)
        phase_c(nc, io, w, scr)


def kernel(**inputs):
    import numpy as np
    import concourse.bacc as bacc
    from concourse.bass_utils import run_bass_kernel_spmd

    a = {n: np.asarray(v) for n, v in inputs.items()}
    ctx = a["ctx_1024"]
    arrays = {
        "x": a["x"].reshape(TOK, D),
        "ctx": ctx.reshape(B, KEYS, C, P).transpose(0, 3, 2, 1),
        "ctx_last": ctx[:, NK].reshape(B, C, P).transpose(2, 1, 0),
        "mask": a["mask_BxSxS2_ik0"].reshape(PAIRS, 2, S, KEYS).transpose(0, 2, 1, 3),
        "wqkv": a["L0_attn_Wqkv"].reshape(3, D, D).transpose(0, 2, 1),
        "wout": a["L0_attn_Wout"].T,
        "W": a["L0_ffn_W"], "b": a["L0_ffn_b"],
        "logits": a["L0_ffn_logits"].reshape(1, OPS), "u": a["L0_ffn_u"].reshape(1, OPS),
    }
    for n in ("Wq", "Wk", "Wv", "Wo"):
        arrays[n] = a["L0_xattn_" + n]
    for n in ("bq", "bk", "bv"):
        arrays[n] = a["L0_xattn_" + n].reshape(C, P).T
    arrays["bo"] = a["L0_xattn_bo"]
    arrays = {f"{n}_dram": np.ascontiguousarray(v) for n, v in arrays.items()}

    nc = bacc.Bacc("TRN2", target_bir_lowering=False, num_devices=1)
    t = {n[:-5]: nc.dram_tensor(n, v.shape, mybir.dt.from_np(v.dtype), kind="ExternalInput").ap()
         for n, v in arrays.items()}
    out = nc.dram_tensor("out_dram", (TOK, D), F32, kind="ExternalOutput").ap()
    io = dict(t)
    io["x"] = t["x"].rearrange("(s t p) n -> s t p n", s=NSUP, t=TILES)
    io["x_tiles"] = t["x"].rearrange("(k p) n -> k p n", p=P)
    io["out"] = out.rearrange("(s t p) n -> s p t n", s=NSUP, t=TILES)
    io["wqkv"] = t["wqkv"].rearrange("m (c p) n -> m p c n", p=P)
    io["W"] = t["W"].rearrange("m (c p) n -> m p c n", p=P)
    io["wout"] = t["wout"].rearrange("(c p) n -> p c n", p=P)
    for n in ("Wq", "Wk", "Wv", "Wo"):
        io[n] = t[n].rearrange("(c p) n -> p c n", p=P)
    program(nc, io)
    r = run_bass_kernel_spmd(nc, [arrays], core_ids=[0])
    return r.results[0]["out_dram"].reshape(B, S, D)
```

```python
import math
from contextlib import ExitStack

import concourse.bass as bass
from concourse import mybir

F32 = mybir.dt.float32
F32R = mybir.dt.float32r
I32 = mybir.dt.int32
U32 = mybir.dt.uint32
ALU = mybir.AluOpType
ACT = mybir.ActivationFunctionType
AX = mybir.AxisListType

P = 128
B, S, D, H = 128, 32, 512, 16
DK = D // H
KEYS = 257
NK = KEYS - 1
C = D // P
HG = P // DK
TOK = B * S
SUP = 512
NSUP = TOK // SUP
TILES = SUP // P
PAIRS = B // 2
QUADS = B // 4
OPS = 8
SCALE = float(DK) ** -0.5
EPS = 1e-5
MASKED = -1e30
FAR = 3.0e38


def wait(eng, sem, value):
    if not (isinstance(value, int) and value <= 0):
        eng.wait_ge(sem, value)


def product3(eng, out, w_hi, w_lo, m_hi, m_lo):
    last = None
    for c in range(C):
        for k, (w, m) in enumerate(((w_hi, m_hi), (w_hi, m_lo), (w_lo, m_hi))):
            last = eng.matmul(out, w(c), m(c), start=(c == 0 and k == 0), stop=(c == C - 1 and k == 2))
    return last


def inverse_deviation(dve, x, w, step_sem, base, tiles=range(TILES)):
    stats, mv, small = w["stats"], w["mv"], w["small"]
    span = slice(tiles[0], tiles[-1] + 1)
    v, y, t2 = small[:, 0, span], small[:, 1, span], small[:, 2, span]
    for t in tiles:
        i = dve.bn_stats(stats[:, t, :], x[:, t, :])
    i.then_inc(step_sem, 1)
    dve.wait_ge(step_sem, base + 1)
    dve.memset(w["gate"][:], 0.0)
    for t in tiles:
        i = dve.bn_aggr(mv[:, t, :], stats[:, t, :])
    i.then_inc(step_sem, 1)
    dve.wait_ge(step_sem, base + 2)
    dve.tensor_scalar(v, mv[:, span, 1], EPS, None, ALU.add).then_inc(step_sem, 1)
    dve.wait_ge(step_sem, base + 3)
    dve.tensor_scalar(y.bitcast(I32), v.bitcast(I32), -0.5, MAGIC, ALU.mult, ALU.add).then_inc(step_sem, 1)
    for k in range(NEWTON):
        dve.wait_ge(step_sem, base + (4 + 3 * k))
        dve.scalar_tensor_tensor(t2, v, -0.5, y, ALU.mult, ALU.mult).then_inc(step_sem, 1)
        dve.wait_ge(step_sem, base + (5 + 3 * k))
        dve.tensor_tensor(t2, t2, y, ALU.mult).then_inc(step_sem, 1)
        dve.wait_ge(step_sem, base + (6 + 3 * k))
        dve.scalar_tensor_tensor(y, t2, 1.5, y, ALU.add, ALU.mult).then_inc(step_sem, 1)


def normalise(dve, x, xn, w, done, step_sem, base, tiles=range(TILES)):
    dve.wait_ge(step_sem, base + LN_STEPS)
    for t in tiles:
        i = dve.tensor_scalar(xn[:, t, :], x[:, t, :], w["mv"][:, t, 0:1], w["small"][:, 1, t:t + 1],
                              ALU.subtract, ALU.mult)
    i.then_inc(done, 1)


def layer_norm(dve, x, xn, w, done, step_sem, base, tiles=range(TILES)):
    inverse_deviation(dve, x, w, step_sem, base, tiles)
    normalise(dve, x, xn, w, done, step_sem, base, tiles)


MAGIC = 1597463007.0
NEWTON = 3
LN_STEPS = 4 + 3 * NEWTON


def split_context(dve, w, p, par, h):
    raw = w["ctx"][:, par, h]
    keys = slice(h * NK, (h + 1) * NK)
    for c in range(C):
        i = dve.tensor_scalar(w["split_hi"][:, par, c, keys], raw[:, c, 0:NK], raw[:, c, NK:KEYS],
                              None, ALU.subtract)
    i.then_inc(w["cx_hi_done"], 1)
    dve.wait_ge(w["cx_hi_done"], p * 2 + (h + 1))
    for c in range(C):
        i = dve.scalar_tensor_tensor(w["split_lo"][:, par, c, keys], raw[:, c, 0:NK], raw[:, c, NK:KEYS],
                                     w["split_hi"][:, par, c, keys].bitcast(F32), ALU.subtract, ALU.subtract)
    i.then_inc(w["cx_done"], 1)


def load_context(sp, io, w, p, par):
    for h in range(2):
        sp.dma_start(w["ctx"][:, par, h], io["ctx"][p * 2 + h]).then_inc(w["ctx_in"][par], 16)


def self_weight_high(act, w, n):
    act.wait_ge(w["w_in"][n], 16)
    act.copy(w["c_hi"][n].rearrange("p c n -> p (c n)"),
             w["staging"][n].rearrange("p c n -> p (c n)")).then_inc(w["w_hi_done"], 1)


def self_weight_low(dve, w, n):
    dve.wait_ge(w["w_hi_done"], n + 1)
    dve.tensor_tensor(w["c_lo"][n].rearrange("p c n -> p (c n)"), w["staging"][n].rearrange("p c n -> p (c n)"),
                      w["c_hi"][n].bitcast(F32).rearrange("p c n -> p (c n)"),
                      ALU.subtract).then_inc(w["w_lo_done"], 1)


def phase_a(nc, io, w, scr):
    with ExitStack() as ctx:
        def sb(name, shape, dt=F32):
            return ctx.enter_context(nc.sbuf_tensor("a_" + name, shape, dt))

        def sem(name):
            return ctx.enter_context(nc.semaphore("a_" + name))

        raw = sb("raw", [P, 4, C, D])
        wq_hi = sb("wq_hi", [P, C, D], F32R)
        wq_lo = sb("wq_lo", [P, C, D], F32R)
        last_t = sb("last_t", [P, C, B])
        bq = sb("bq", [P, C])
        bqs = sb("bqs", [P, C])
        bv = sb("bv", [P, C])
        x = sb("x", [P, 2, TILES, D])
        xt_hi, xt_lo = w["split_hi"], w["split_lo"]
        q = w["v"][:].rearrange("p s b (a g t) -> p s (b a) g t", g=C, t=64)
        pick = sb("pick", [1, 8, OPS])
        best = sb("best", [1, OPS])
        ps = ctx.enter_context(nc.psum_tensor("a_ps", [P, 8, 512], F32))
        PROJ, TRN, VL = (0, 1), (2, 3, 4, 5), 6

        weights_in = [sem(f"weights_in{k}") for k in range(4)]
        consts_in, last_in, pick_in = sem("consts_in"), sem("last_in"), sem("pick_in")
        pick_act, pick_dve = sem("pick_act"), sem("pick_dve")
        x_in = [sem("x_in0"), sem("x_in1")]
        hi_done, lo_done = sem("hi_done"), sem("lo_done")
        bqs_done = sem("bqs_done")
        vl_mm, vl_done = sem("vl_mm"), sem("vl_done")
        step_sem, xn_done = sem("ln_step"), sem("xn_done")
        transposed = sem("transposed")
        xt_hi_done, xt_lo_done = sem("xt_hi_done"), sem("xt_lo_done")
        q_mm, q_evac = sem("q_mm"), sem("q_evac")
        q_stored = w["q_stored"]
        block = ctx.enter_context(nc.Block())
        hi = (wq_hi, w["wk_hi"], w["wv_hi"], w["wo_hi"])
        lo = (wq_lo, w["wk_lo"], w["wv_lo"], w["wo_lo"])

        @block.sync
        def _(sp):
            def load(s, par):
                wait(sp, transposed, 4 * (s - 1))
                sp.dma_start(x[:, par], io["x"][s].rearrange("t p n -> p t n")).then_inc(x_in[par], 16)

            def store(s, par):
                sp.wait_ge(q_evac, s * 4 + 4)
                sp.dma_start(scr["q"][s].rearrange("a p n -> p a n"),
                             q[:, par].rearrange("p a g t -> p a (g t)")).then_inc(q_stored[par], 16)

            load(0, 0)
            sp.dma_start(pick[:, 0, :], io["logits"]).then_inc(pick_in, 16)
            sp.dma_start(pick[:, 1, :], io["u"]).then_inc(pick_in, 16)
            names = ("Wq", "Wk", "Wv", "Wo")
            sp.dma_start(raw[:, 0], io["Wq"]).then_inc(weights_in[0], 16)
            sp.dma_start(bq[:], io["bq"]).then_inc(consts_in, 16)
            sp.dma_start(bv[:], io["bv"]).then_inc(consts_in, 16)
            sp.dma_start(w["bk"][:], io["bk"]).then_inc(consts_in, 16)
            load(1, 1)
            for k in (2, 1, 3):
                sp.dma_start(raw[:, k], io[names[k]]).then_inc(weights_in[k], 16)
            sp.dma_start(last_t[:], io["ctx_last"]).then_inc(last_in, 16)
            load(2, 0)
            load(3, 1)
            store(0, 0)
            load(4, 0)
            store(1, 1)
            with sp.Fori(1, NSUP // 2 - 2) as i:
                load(i * 2 + 3, 1)
                store(i * 2, 0)
                load(i * 2 + 4, 0)
                store(i * 2 + 1, 1)
            load(NSUP - 1, 1)
            store(NSUP - 4, 0)
            load_context(sp, io, w, 0, 0)
            store(NSUP - 3, 1)
            load_context(sp, io, w, 1, 1)
            store(NSUP - 2, 0)
            store(NSUP - 1, 1)
            sp.wait_ge(q_stored[0], 16 * (NSUP // 2))
            sp.wait_ge(q_stored[1], 16 * (NSUP // 2 - 1))

        CHUNKS_AFTER = ((0, 1), (2, 3), (), ())

        def steps(eng, step, before_last, loop):
            step(0, 0)
            step(1, 1)
            with eng.Fori(1, NSUP // 2 - 1) as i:
                loop[0] = i
                step(i * 2, 0)
                step(i * 2 + 1, 1)
            step(NSUP - 2, 0, norm=False)
            before_last()
            step(NSUP - 1, 1, norm=False, turn=False)

        @block.scalar
        def _(act):
            def high(s, par, c):
                act.wait_ge(transposed, s * 4 + (c + 1))
                if c == 0:
                    wait(act, q_mm, (s - 1) * 4)
                act.copy(xt_hi[:, par, c, :], ps[:, TRN[c], :]).then_inc(xt_hi_done, 1)

            def weight(k):
                act.wait_ge(weights_in[k], 16)
                act.copy(hi[k][:], raw[:, k]).then_inc(hi_done, 1)

            def step(s, par, norm=True, turn=True):
                if isinstance(s, int) and s < 2:
                    weight((2, 1)[s])
                for g in range(C):
                    act.wait_ge(q_mm, s * 4 + (g + 1))
                    if g == 0:
                        wait(act, q_stored[par], stored_before(s))
                    act.activation(q[:, par, :, g, :], ps[:, PROJ[g % 2], :].rearrange("p (a t) -> p a t", t=64),
                                   ACT.Identity, bias=bqs[:, g:g + 1], scale=SCALE).then_inc(q_evac, 1)
                    if turn:
                        for c in CHUNKS_AFTER[g]:
                            high(s + 1, 1 - par, c)

            def select():
                act.wait_ge(pick_in, 32)
                act.activation(pick[:, 6, :], pick[:, 1, :], ACT.Ln).then_inc(pick_act, 1)
                act.wait_ge(pick_act, 1)
                act.activation(pick[:, 1, :], pick[:, 6, :], ACT.Ln, scale=-1.0).then_inc(pick_act, 1)
                act.wait_ge(pick_dve, 2)
                act.activation(pick[:, 4, :], pick[:, 0, :], ACT.Exp, bias=pick[:, 3, 0:1],
                               accum_out=pick[:, 5, 0:1]).then_inc(pick_act, 1)
                act.wait_ge(pick_act, 3)
                act.activation(pick[:, 6, 0:1], pick[:, 5, 0:1], ACT.Ln).then_inc(pick_act, 1)

            select()
            weight(0)
            for c in range(C):
                high(0, 0, c)
            act.wait_ge(bqs_done, 1)
            loop = [None]

            def stored_before(s):
                return s // 2 * 16 if isinstance(s, int) else loop[0] * 16

            steps(act, step, lambda: weight(3), loop)

        @block.vector
        def _(dve):
            def ln_start(s, par, nth):
                dve.wait_ge(x_in[par], nth * 16)
                inverse_deviation(dve, x[:, par], w, step_sem, s * LN_STEPS)

            def ln_end(s, par):
                normalise(dve, x[:, par], x[:, par], w, xn_done, step_sem, s * LN_STEPS)

            def lows(s, par, chunks=range(C)):
                for c in chunks:
                    dve.wait_ge(xt_hi_done, s * 4 + (c + 1))
                    dve.tensor_tensor(xt_lo[:, par, c, :], ps[:, TRN[c], :], xt_hi[:, par, c, :].bitcast(F32),
                                      ALU.subtract).then_inc(xt_lo_done, 1)

            def step(s, par, norm=True):
                if norm:
                    ln_start(s + 2, par, s // 2 + 2 if isinstance(s, int) else nth[0])
                lows(s + 1, 1 - par, (0, 1))
                if norm:
                    ln_end(s + 2, par)
                lows(s + 1, 1 - par, (2, 3))

            def last_values():
                dve.wait_ge(vl_mm, 1)
                for g in range(C):
                    i = dve.tensor_scalar(w["v_last"][:, :, g], ps[:, VL, g * B:(g + 1) * B], bv[:, g:g + 1],
                                          None, ALU.add)
                i.then_inc(vl_done, 1)

            def largest_logit():
                dve.wait_ge(pick_in, 32)
                dve.tensor_reduce(pick[:, 2, 0:1], pick[:, 0, :], AX.X, ALU.max).then_inc(pick_dve, 1)
                dve.wait_ge(pick_dve, 1)
                dve.tensor_scalar(pick[:, 3, 0:1], pick[:, 2, 0:1], -1.0, None, ALU.mult).then_inc(pick_dve, 1)

            def select():
                dve.wait_ge(pick_act, 4)
                dve.tensor_scalar(pick[:, 7, :], pick[:, 0, :], pick[:, 2, 0:1], pick[:, 6, 0:1], ALU.subtract,
                                  ALU.subtract).then_inc(pick_dve, 1)
                dve.wait_ge(pick_dve, 3)
                dve.tensor_tensor(pick[:, 4, :], pick[:, 7, :], pick[:, 1, :], ALU.subtract).then_inc(pick_dve, 1)
                dve.wait_ge(pick_dve, 4)
                dve.max(best[:], pick[:, 4, :]).then_inc(pick_dve, 1)
                dve.wait_ge(pick_dve, 5)
                dve.max_index(w["choice"][:], best[:], pick[:, 4, :]).then_inc(pick_dve, 1)

            nth = [None]
            largest_logit()
            ln_start(0, 0, 1)
            ln_end(0, 0)
            select()
            dve.wait_ge(consts_in, 48)
            dve.tensor_scalar(bqs[:], bq[:], SCALE, None, ALU.mult).then_inc(bqs_done, 1)
            ln_start(1, 1, 1)
            lows(0, 0)
            ln_end(1, 1)
            step(0, 0)
            step(1, 1)
            with dve.Fori(1, NSUP // 2 - 1) as i:
                nth[0] = i + 2
                step(i * 2, 0)
                step(i * 2 + 1, 1)
            step(NSUP - 2, 0, norm=False)
            last_values()
            dve.wait_ge(q_mm, (NSUP - 1) * 4)
            dve.wait_ge(w["ctx_in"][0], 32)
            split_context(dve, w, 0, 0, 0)
            split_context(dve, w, 0, 0, 1)

        @block.tensor
        def _(pe):
            def turn_chunk(s, par, c):
                if c == 0:
                    pe.wait_ge(xn_done, s + 1)
                wait(pe, xt_lo_done, s * 4 + (c - 3))
                for t in range(TILES):
                    i = pe.transpose(ps[:, TRN[c], t * P:(t + 1) * P], x[:, par, t, c * P:(c + 1) * P],
                                     w["ident"][:])
                i.then_inc(transposed, 1)

            def step(s, par, norm=True, turn=True):
                pe.wait_ge(xt_lo_done, s * 4 + 4)
                for g in range(C):
                    wait(pe, q_evac, s * 4 + (g - 1))
                    product3(pe, ps[:, PROJ[g % 2], :],
                             lambda c: wq_hi[:, c, g * P:(g + 1) * P], lambda c: wq_lo[:, c, g * P:(g + 1) * P],
                             lambda c: xt_hi[:, par, c, :], lambda c: xt_lo[:, par, c, :]).then_inc(q_mm, 1)
                    if turn:
                        for c in CHUNKS_AFTER[g]:
                            turn_chunk(s + 1, 1 - par, c)

            def last_values():
                pe.wait_ge(weights_in[2], 16)
                pe.wait_ge(last_in, 16)
                for g in range(C):
                    for c in range(C):
                        i = pe.matmul(ps[:, VL, g * B:(g + 1) * B], raw[:, 2, c, g * P:(g + 1) * P],
                                      last_t[:, c, :], start=(c == 0), stop=(c == C - 1))
                i.then_inc(vl_mm, 1)

            pe.wait_ge(w["ident_ready"], 2)
            for c in range(C):
                turn_chunk(0, 0, c)
            pe.wait_ge(lo_done, 1)
            steps(pe, step, last_values, [None])

        @block.gpsimd
        def _(pool):
            pool.memset(w["ident"][:], 0.0).then_inc(w["ident_ready"], 1)
            pool.wait_ge(w["ident_ready"], 1)
            pool.affine_select(out=w["ident"][:], in_=w["ident"][:], compare_op=ALU.not_equal, fill=1.0,
                               base=0, pattern=[[-1, P]], channel_multiplier=1).then_inc(w["ident_ready"], 1)
            for n, k in enumerate((0, 2, 1, 3)):
                pool.wait_ge(hi_done, n + 1)
                pool.tensor_tensor(lo[k][:], raw[:, k], hi[k][:].bitcast(F32), ALU.subtract).then_inc(lo_done, 1)


def phase_b(nc, io, w, scr):
    with ExitStack() as ctx:
        def sb(name, shape, dt=F32):
            return ctx.enter_context(nc.sbuf_tensor("b_" + name, shape, dt))

        def sem(name):
            return ctx.enter_context(nc.semaphore("b_" + name))

        cx_hi, cx_lo = w["split_hi"], w["split_lo"]
        kt_hi = sb("kt_hi", [P, 2, C, 2, KEYS + 1], F32R)
        kt_lo = sb("kt_lo", [P, 2, C, 2, KEYS + 1], F32R)
        v = w["v"]
        mask_raw = sb("mask_raw", [P, 2, KEYS], I32)
        mask = sb("mask", [P, 2, 2, KEYS])
        qt = sb("qt", [P, 2, C, 64])
        qb_hi = sb("qb_hi", [P, 2, C, P], F32R)
        qb_lo = sb("qb_lo", [P, 2, C, P], F32R)
        sm = sb("sm", [P, 2, C, KEYS])
        pr = sb("pr", [P, 2, C, KEYS])
        low = sb("low", [P, 2, C])
        rsum = sb("rsum", [P, 2, C])
        rinv = sb("rinv", [P, 2, C])
        pt = sb("pt", [P, 2, 2, D])
        ot = sb("ot", [P, C, P])
        ot_hi = sb("ot_hi", [P, C, P], F32R)
        ot_lo = sb("ot_lo", [P, C, P], F32R)
        x = sb("x", [P, D])
        x2 = w["row"]
        bo = sb("bo", [P, D])
        gate = sb("gates", [1, 2 * C])
        one = sb("one", [P, 1])
        ps = ctx.enter_context(nc.psum_tensor("b_ps", [P, 8, 512], F32))
        PROJ, SC, PT, OUT = (0, 1), (2, 3, 4), (5, 6), 7

        q_in = [sem("q_in0"), sem("q_in1")]
        mask_in, x_in, bo_in = sem("mask_in"), sem("x_in"), sem("bo_in")
        zeroed, bk_ready = sem("zeroed"), sem("bk_ready")
        qb_hi_done = sem("qb_hi_done")
        mask_ready, qb_ready = sem("mask_ready"), sem("qb_ready")
        ctx_in, cx_done = w["ctx_in"], w["cx_done"]
        proj_mm = sem("proj_mm")
        k_hi_done, k_done, v_done = sem("k_hi_done"), sem("k_done"), sem("v_done")
        sc_mm, masked, exp_done = sem("sc_mm"), sem("masked"), sem("exp_done")
        inv_done, norm_done = sem("inv_done"), sem("norm_done")
        pt_mm, pt_evac = sem("pt_mm"), sem("pt_evac")
        pv_mm, o_done = sem("pv_mm"), sem("o_done")
        ot_hi_done, ot_done = sem("ot_hi_done"), sem("ot_done")
        op_mm, xb_done, x2_done, x2_stored = sem("op_mm"), sem("xb_done"), sem("x2_done"), w["x2_stored"]
        block = ctx.enter_context(nc.Block())

        SCORES_AFTER = ((0, (0, 1)), (0, (2, 3)), (1, (0, 1)), (1, (2, 3)))

        def bank(g, h, par):
            return SC[(h * C + g + (2 if par else 0)) % 3]

        FIRST, LAST = 1, PAIRS // 2 - 1

        @block.sync
        def _(sp):
            def load_ctx(p, par):
                wait(sp, cx_done, (p - 1) * 2)
                load_context(sp, io, w, p, par)

            def load_small(p, par):
                wait(sp, mask_ready, p)
                for j in range(HG):
                    sp.dma_start(mask_raw[j * S:(j + 1) * S], io["mask"][p]).then_inc(mask_in, 16)
                wait(sp, qb_ready, (p - 1) * 8)
                sp.dma_start(qt[:, par], scr["q_pairs"][p]).then_inc(q_in[par], 16)

            def residual_in(k):
                wait(sp, x2_done, k)
                sp.dma_start(x[:], io["x_tiles"][k]).then_inc(x_in, 16)

            def result_out(k):
                sp.wait_ge(x2_done, k + 1)
                sp.dma_start(scr["x2"][k], x2[:]).then_inc(x2_stored, 16)

            def quad_io(k):
                residual_in(k)
                result_out(k)

            sp.dma_start(bo[:], io["bo"].partition_broadcast(P)).then_inc(bo_in, 16)
            load_small(0, 0)
            sp.wait_ge(w["q_stored"][1], 16 * (NSUP // 2))
            for p in range(3):
                load_ctx(p + 2, p % 2)
                load_small(p + 1, 1 - p % 2)
            quad_io(0)
            with sp.Fori(FIRST, LAST - 1) as i:
                load_ctx(i * 2 + 3, 1)
                load_small(i * 2 + 2, 0)
                load_ctx(i * 2 + 4, 0)
                load_small(i * 2 + 3, 1)
                quad_io(i)
            load_ctx(PAIRS - 1, 1)
            load_small(PAIRS - 2, 0)
            load_small(PAIRS - 1, 1)
            sp.wait_ge(cx_done, (PAIRS - 1) * 2)
            sp.wait_ge(x2_stored, 16 * TILES)
            sp.dma_start(w["xl"], scr["x2_sup"][0]).then_inc(w["xl_in"], 16)
            quad_io(QUADS - 2)
            residual_in(QUADS - 1)
            sp.wait_ge(cx_done, PAIRS * 2)
            sp.dma_start(w["staging"][0], io["wqkv"][0]).then_inc(w["w_in"][0], 16)
            sp.wait_ge(pv_mm, (PAIRS - 1) * 2)
            sp.dma_start(w["staging"][1], io["wqkv"][1]).then_inc(w["w_in"][1], 16)
            result_out(QUADS - 1)

        @block.gpsimd
        def _(pool):
            def expand(p, par, h, nth):
                if h == 0:
                    pool.wait_ge(q_in[par], nth * 16)
                wait(pool, sc_mm, (p * 2 + (h - 1)) * 4)
                for j in range(HG):
                    r = slice(j * DK, (j + 1) * DK)
                    pool.tensor_tensor(qb_hi[r, h, :, r], qt[r, par, :, h * S:(h + 1) * S],
                                       one[r].unsqueeze(1).to_broadcast([DK, C, S]), ALU.mult).then_inc(qb_hi_done, 1)
                for j in range(HG):
                    r = slice(j * DK, (j + 1) * DK)
                    pool.wait_ge(qb_hi_done, (p * 2 + h) * 4 + (j + 1))
                    pool.tensor_tensor(qb_lo[r, h, :, r], qt[r, par, :, h * S:(h + 1) * S],
                                       qb_hi[r, h, :, r].bitcast(F32), ALU.subtract).then_inc(qb_ready, 1)

            pool.memset(qb_hi[:].bitcast(F32), 0.0).then_inc(zeroed, 1)
            pool.memset(qb_lo[:].bitcast(F32), 0.0).then_inc(zeroed, 1)
            pool.memset(one[:], 1.0).then_inc(zeroed, 1)
            pool.wait_ge(zeroed, 3)
            for p in range(3):
                expand(p, p % 2, 0, p // 2 + 1)
                expand(p, p % 2, 1, p // 2 + 1)
            with pool.Fori(FIRST, LAST) as i:
                for n, par in ((1, 1), (2, 0)):
                    p = i * 2 + n
                    expand(p, par, 0, i + n)
                    expand(p, par, 1, i + n)
            p = PAIRS - 1
            expand(p, 1, 0, PAIRS // 2)
            expand(p, 1, 1, PAIRS // 2)

        @block.scalar
        def _(act):
            def step(p, par, attend=True, project=True, ahead=True):
                def evac(n):
                    if not project:
                        return
                    act.wait_ge(proj_mm, p * 8 + (n + 1))
                    if n < 4:
                        if n == 0:
                            wait(act, sc_mm, (p - 1) * 8)
                        act.activation(kt_hi[:, par, n, :, 0:NK], ps[:, PROJ[n % 2], :].rearrange(
                            "p (h k) -> p h k", h=2), ACT.Identity, bias=w["bk"][:, n:n + 1]).then_inc(k_hi_done, 1)
                    else:
                        if n == 4:
                            wait(act, pv_mm, (p - 1) * 2)
                            if isinstance(p, int) and p == 1:
                                act.wait_ge(w["q_stored"][1], 16 * (NSUP // 2))
                        act.copy(v[:, par, n - 4, :], ps[:, PROJ[n % 2], :]).then_inc(v_done, 1)

                def exps(h, groups):
                    if not attend:
                        return
                    b = (p - 1) * 2 + h
                    if groups[0] == 0:
                        wait(act, pt_mm, (b - 1) * 2)
                    for g in groups:
                        act.wait_ge(masked, b * 4 + (g + 1))
                        act.activation(pr[:, h, g, :], sm[:, h, g, :], ACT.Exp, bias=low[:, h, g:g + 1],
                                       scale=-1.0, accum_out=rsum[:, h, g:g + 1]).then_inc(exp_done, 1)

                def pt_out(h):
                    if not attend:
                        return
                    b = (p - 1) * 2 + h
                    for kc in range(2):
                        act.wait_ge(pt_mm, b * 2 + (kc + 1))
                        if kc == 0:
                            wait(act, pv_mm, b - 1)
                        act.copy(pt[:, h, kc, :], ps[:, PT[kc], :]).then_inc(pt_evac, 1)

                for n in range(4):
                    evac(n)
                    exps(*SCORES_AFTER[n])
                pt_out(0)
                evac(4)
                evac(5)
                pt_out(1)
                evac(6)
                evac(7)
                if not project:
                    act.wait_ge(proj_mm, PAIRS * 8)
                    self_weight_high(act, w, 0)
                    self_weight_high(act, w, 1)

            step(0, 0, attend=False)
            step(1, 1)
            step(2, 0)
            with act.Fori(FIRST, LAST) as i:
                step(i * 2 + 1, 1)
                step(i * 2 + 2, 0)
            step(PAIRS - 1, 1)
            step(PAIRS, 0, project=False)

        @block.vector
        def _(dve):
            def split(p, par, h):
                if h == 0:
                    wait(dve, proj_mm, (p - 1) * 8)
                    dve.wait_ge(ctx_in[par], in_count(p))
                split_context(dve, w, p, par, h)

            loop = [None]

            def in_count(p):
                return 32 * (p // 2 + 1) if isinstance(p, int) else loop[0] * 32 + 64

            def step(p, par, attend=True, project=True, ahead=True):
                def mask_rows(h, groups):
                    if not attend:
                        return
                    b = (p - 1) * 2 + h
                    if groups[0] == 0:
                        if h == 0:
                            dve.wait_ge(mask_ready, p)
                        wait(dve, exp_done, (b - 1) * 4)
                    for g in groups:
                        dve.wait_ge(sc_mm, b * 4 + (g + 1))
                        dve.memset(gate[:, h * C + g:h * C + g + 1], 0.0)
                        dve.tensor_tensor_reduce(sm[:, h, g, :], ps[:, bank(g, h, par), 0:KEYS],
                                                 mask[:, 1 - par, h, :], -1.0, FAR, ALU.add, ALU.min,
                                                 low[:, h, g:g + 1]).then_inc(masked, 1)

                def k_low(n):
                    if not project:
                        return
                    dve.wait_ge(k_hi_done, p * 4 + (n + 1))
                    dve.scalar_tensor_tensor(kt_lo[:, par, n, :, 0:NK], ps[:, PROJ[n % 2], :].rearrange(
                        "p (h k) -> p h k", h=2), w["bk"][:, n:n + 1], kt_hi[:, par, n, :, 0:NK].bitcast(F32),
                        ALU.add, ALU.subtract).then_inc(k_done, 1)

                def norm(h):
                    if not attend:
                        return
                    b = (p - 1) * 2 + h
                    dve.wait_ge(exp_done, b * 4 + 4)
                    dve.reciprocal(rinv[:, h, :], rsum[:, h, :]).then_inc(inv_done, 1)
                    dve.wait_ge(inv_done, b + 1)
                    for g in range(C):
                        i = dve.tensor_scalar(pr[:, h, g, 0:NK], pr[:, h, g, 0:NK], rinv[:, h, g:g + 1], None,
                                              ALU.mult)
                    i.then_inc(norm_done, 1)

                def out(h):
                    if not attend:
                        return
                    b = (p - 1) * 2 + h
                    at = (2 * (1 - par) + h) * S
                    dve.wait_ge(pv_mm, b + 1)
                    dve.tensor_tensor(ot[:, :, at:at + S], ps[:, OUT, 0:P].rearrange("p (g q) -> p g q", g=C),
                                      w["v_last"][:, b, :].unsqueeze(2).to_broadcast([P, C, S]),
                                      ALU.add).then_inc(o_done, 1)

                def quad_out():
                    k = p // 2 - 1 if isinstance(p, int) else loop[0]
                    dve.wait_ge(o_done, k * 4 + 4)
                    wait(dve, op_mm, k)
                    dve.tensor_copy(ot_hi[:], ot[:]).then_inc(ot_hi_done, 1)
                    dve.wait_ge(ot_hi_done, k + 1)
                    dve.tensor_tensor(ot_lo[:], ot[:], ot_hi[:].bitcast(F32), ALU.subtract).then_inc(ot_done, 1)
                    if not project:
                        self_weight_low(dve, w, 0)
                        self_weight_low(dve, w, 1)
                    dve.wait_ge(x_in, k * 16 + 16)
                    dve.tensor_tensor(x[:], x[:], bo[:], ALU.add).then_inc(xb_done, 1)
                    dve.wait_ge(xb_done, k + 1)
                    wait(dve, x2_stored, k * 16)
                    dve.wait_ge(op_mm, k + 1)
                    dve.tensor_tensor(x2[:], ps[:, OUT, :], x[:], ALU.add).then_inc(x2_done, 1)

                for n in range(4):
                    k_low(n)
                    mask_rows(*SCORES_AFTER[n])
                    if n == 0 and project:
                        dve.wait_ge(mask_in, p * 64 + 64)
                        dve.tensor_scalar(mask[:, par], mask_raw[:], 0.0, MASKED, ALU.is_equal,
                                          ALU.mult).then_inc(mask_ready, 1)
                    if n == 2:
                        norm(0)
                if ahead:
                    split(p + 1, 1 - par, 0)
                norm(1)
                out(0)
                if ahead:
                    split(p + 1, 1 - par, 1)
                elif project:
                    dve.wait_ge(w["xl_in"], 16)
                    layer_norm(dve, w["xl"], w["xl"], w, w["xn2_done"], w["ln2_step"], 0)
                out(1)
                if attend and par == 0:
                    quad_out()

            bk_cols = w["bk"][:].unsqueeze(2).unsqueeze(3).to_broadcast([P, C, 2, 2])
            for par in range(2):
                dve.tensor_copy(kt_hi[:, par, :, :, NK:], bk_cols).then_inc(bk_ready, 1)
            dve.wait_ge(bk_ready, 2)
            for par in range(2):
                dve.tensor_tensor(kt_lo[:, par, :, :, NK:], bk_cols, kt_hi[:, par, :, :, NK:].bitcast(F32),
                                  ALU.subtract).then_inc(bk_ready, 1)
            dve.wait_ge(bo_in, 16)
            step(0, 0, attend=False)
            step(1, 1)
            step(2, 0)
            with dve.Fori(FIRST, LAST) as i:
                loop[0] = i
                step(i * 2 + 1, 1)
                step(i * 2 + 2, 0)
            step(PAIRS - 1, 1, ahead=False)
            step(PAIRS, 0, project=False, ahead=False)

        @block.tensor
        def _(pe):
            def step(p, par, attend=True, project=True, ahead=True):
                def project_block(n):
                    if not project:
                        return
                    if n == 0:
                        pe.wait_ge(cx_done, p * 2 + 2)
                    if n < 2:
                        wait(pe, v_done, p * 4 + (n - 1))
                    elif n < 6:
                        pe.wait_ge(k_done, p * 4 + (n - 1))
                    else:
                        pe.wait_ge(v_done, p * 4 + (n - 5))
                    out = ps[:, PROJ[n % 2], :]
                    if n < 4:
                        r = slice(n * P, (n + 1) * P)
                        i = product3(pe, out, lambda c: w["wk_hi"][:, c, r], lambda c: w["wk_lo"][:, c, r],
                                     lambda c: cx_hi[:, par, c, :], lambda c: cx_lo[:, par, c, :])
                    else:
                        r = slice((n - 4) * P, (n - 3) * P)
                        i = product3(pe, out, lambda c: cx_hi[:, par, c, r], lambda c: cx_lo[:, par, c, r],
                                     lambda c: w["wv_hi"][:, c, :], lambda c: w["wv_lo"][:, c, :])
                    i.then_inc(proj_mm, 1)

                def scores(h, groups):
                    if not attend:
                        return
                    b = (p - 1) * 2 + h
                    if groups[0] == 0:
                        pe.wait_ge(qb_ready, b * 4 + 4)
                        if h == 0:
                            pe.wait_ge(k_done, p * 4)
                    for g in groups:
                        first = par == 0 and h == 0 and g == 0
                        wait(pe, masked, b * 4 if first else b * 4 + (g - 2))
                        out = ps[:, bank(g, h, par), 0:KEYS + 1]
                        k_hi, k_lo = kt_hi[:, 1 - par, g, h, :], kt_lo[:, 1 - par, g, h, :]
                        pe.matmul(out, qb_hi[:, h, g, :], k_hi, start=True, stop=False)
                        pe.matmul(out, qb_hi[:, h, g, :], k_lo, start=False, stop=False)
                        pe.matmul(out, qb_lo[:, h, g, :], k_hi, start=False, stop=True).then_inc(sc_mm, 1)

                def transposes(h):
                    if not attend:
                        return
                    b = (p - 1) * 2 + h
                    pe.wait_ge(norm_done, b + 1)
                    for kc in range(2):
                        wait(pe, pt_evac, b * 2 + (kc - 1))
                        for g in range(C):
                            i = pe.transpose(ps[:, PT[kc], g * P:(g + 1) * P], pr[:, h, g, kc * P:(kc + 1) * P],
                                             w["ident"][:])
                        i.then_inc(pt_mm, 1)

                def values(h):
                    if not attend:
                        return
                    b = (p - 1) * 2 + h
                    pe.wait_ge(pt_evac, b * 2 + 2)
                    pe.wait_ge(v_done, p * 4)
                    wait(pe, o_done, b)
                    if par == 1 and h == 0:
                        wait(pe, x2_done, p // 2 if isinstance(p, int) else loop[0])
                    for g in range(C):
                        for kc in range(2):
                            for j in range(HG):
                                f = g * P + j * DK
                                i = pe.matmul(ps[j * DK:(j + 1) * DK, OUT, g * S:(g + 1) * S],
                                              v[:, 1 - par, 2 * h + kc, f:f + DK],
                                              pt[:, h, kc, f:f + DK], start=(kc == 0), stop=(kc == 1))
                    i.then_inc(pv_mm, 1)

                def out_projection():
                    k = p // 2 - 1 if isinstance(p, int) else loop[0]
                    pe.wait_ge(ot_done, k + 1)
                    product3(pe, ps[:, OUT, :], lambda c: ot_hi[:, c, :], lambda c: ot_lo[:, c, :],
                             lambda c: w["wo_hi"][:, c, :], lambda c: w["wo_lo"][:, c, :]).then_inc(op_mm, 1)

                for n in range(4):
                    project_block(n)
                    scores(*SCORES_AFTER[n])
                transposes(0)
                project_block(4)
                values(0)
                project_block(5)
                transposes(1)
                project_block(6)
                values(1)
                project_block(7)
                if attend and par == 0:
                    out_projection()

            loop = [None]
            step(0, 0, attend=False)
            pe.wait_ge(bk_ready, 4)
            step(1, 1)
            step(2, 0)
            with pe.Fori(FIRST, LAST) as i:
                loop[0] = i
                step(i * 2 + 1, 1)
                step(i * 2 + 2, 0)
            step(PAIRS - 1, 1)
            step(PAIRS, 0, project=False)


def phase_c(nc, io, w, scr):
    with ExitStack() as ctx:
        def sb(name, shape, dt=F32):
            return ctx.enter_context(nc.sbuf_tensor("c_" + name, shape, dt))

        def sem(name):
            return ctx.enter_context(nc.semaphore("c_" + name))

        w_hi = [w["c_hi"][0], w["c_hi"][1], sb("wv_hi", [P, C, D], F32R)[:], sb("wout_hi", [P, C, D], F32R)[:],
                w["wo_hi"][:]]
        w_lo = [w["c_lo"][0], w["c_lo"][1], sb("wv_lo", [P, C, D], F32R)[:], sb("wout_lo", [P, C, D], F32R)[:],
                w["wo_lo"][:]]
        xl, res = w["xl"], w["res"]
        xn3 = sb("xn3", [P, TILES, D])[:]
        (xt2_hi, xt2_lo), (xt3_hi, xt3_lo) = ((w["split_hi"][:, k], w["split_lo"][:, k]) for k in range(2))
        BT = P // S
        qb = sb("qb", [P, C, TILES * BT, P])
        k, v = w["v"][:, 0], w["v"][:, 1]
        ex = sb("ex", [P, H, S])
        pr = (sb("pr", [P, H, P]), xn3.rearrange("p t (h q) -> p (t h) q", q=P))
        rden = sb("rden", [P, 2, SUP])
        ot = sb("ot", [P, 2, C, P])
        E_LOW, E_HIGH = math.exp(-10.0), math.exp(10.0)
        causal = sb("causal", [P, P])
        seen = sb("seen", [P, S])
        pool_gate = sb("pool_gate", [1, 1])
        ones = sb("ones", [P, DK])
        bf = w["row"]
        ps = ctx.enter_context(nc.psum_tensor("c_ps", [P, 8, 512], F32))
        PROJ, TRN, SC, OT, DEN = (0, 1), (2, 3), (4, 5), (6, 2), (7, 3, 4, 5)
        w = dict(w, c_hi=w_hi, c_lo=w_lo, staging=w["staging"] + (
            v, pr[0][:].rearrange("p (c h) q -> p c (h q)", c=C), xn3))

        w_in, w_lo_done = w["w_in"], w["w_lo_done"]
        bf_in, xl_in, res_in, stored = sem("bf_in"), w["xl_in"], sem("res_in"), sem("stored")
        consts = sem("consts")
        zeroed = sem("zeroed")
        step2, xn2_done = w["ln2_step"], w["xn2_done"]
        step3, xn3_done = sem("ln3_step"), sem("xn3_done")
        t2_mm, t2_hi, t2_lo = sem("t2_mm"), sem("t2_hi"), sem("t2_lo")
        t3_mm, t3_hi, t3_lo = sem("t3_mm"), sem("t3_hi"), sem("t3_lo")
        qkv_mm, qkv_evac = sem("qkv_mm"), sem("qkv_evac")
        sc_mm, exp_done, clipped, pr_dve = (
            sem(n) for n in ("sc_mm", "exp_done", "clipped", "pr_dve"))
        pr_act = sem("pr_act")
        pv_mm, den_done = sem("pv_mm"), sem("den_done")
        pr_zero = sem("pr_zero")
        o_raw, o_done, o_hi, o_lo = (sem(n) for n in ("o_raw", "o_done", "o_hi", "o_lo"))
        out_mm, x3_done, xb_done, ffn_mm, y_done = (
            sem(n) for n in ("out_mm", "x3_done", "xb_done", "ffn_mm", "y_done"))
        block = ctx.enter_context(nc.Block())

        TURN3 = 7
        LAST = NSUP - 1

        def half_tiles(h):
            return range(2 * h, 2 * h + 2)

        def half_columns(h):
            return slice(2 * h * P, (2 * h + 2) * P)


        def spread(copy, b, t):
            r = slice(b * S, (b + 1) * S)
            return copy(pr[t % 2][r, :, r], ex[r])

        def steps(eng, step):
            step(0, prev=False)
            step(1)
            with eng.Fori(2, NSUP - 1) as s:
                step(s)
            step(NSUP - 1, more=False)

        @block.sync
        def _(sp):
            def load_xl(s):
                wait(sp, t2_mm, s * 4)
                sp.dma_start(xl, scr["x2_sup"][s]).then_inc(xl_in, 16)

            def load_res(s):
                wait(sp, stored, s * 16)
                sp.dma_start(res, scr["x2_sup"][s]).then_inc(res_in, 16)

            def store(s):
                sp.wait_ge(y_done, s * 4 + 4)
                sp.dma_start(io["out"][s], res).then_inc(stored, 16)

            def step(s, prev=True, more=True):
                if more:
                    load_xl(s + 1)
                if prev:
                    store(s - 1)
                load_res(s)

            sp.dma_start(w["staging"][2], io["wqkv"][2]).then_inc(w_in[2], 16)
            sp.dma_start(w["staging"][3], io["wout"]).then_inc(w_in[3], 16)
            chosen = sp.alloc_register("chosen")
            sp.reg_load(chosen, w["choice"][0:1, 0:1])
            choice = sp.snap(chosen, min_val=0, max_val=OPS - 1)
            sp.dma_start(xn3, io["W"][choice]).then_inc(w_in[4], 16)
            sp.wait_ge(w["x2_stored"], 16 * QUADS)
            sp.dma_start(bf[:], io["b"][choice].partition_broadcast(P)).then_inc(bf_in, 16)
            steps(sp, step)
            for h in range(2):
                sp.wait_ge(y_done, (NSUP - 1) * 4 + 2 * (h + 1))
                sp.dma_start(io["out"][NSUP - 1][:, 2 * h:2 * h + 2], res[:, 2 * h:2 * h + 2]).then_inc(stored, 16)
            sp.wait_ge(stored, 16 * (NSUP + 1))

        @block.gpsimd
        def _(pool):
            for g in range(C):
                pool.memset(qb[:, g], 0.0).then_inc(zeroed, 1)
            pool.memset(causal[:], E_HIGH).then_inc(consts, 1)
            pool.memset(ones[:], 1.0).then_inc(consts, 1)
            pool.wait_ge(consts, 2)
            pool.affine_select(out=causal[:], in_=causal[:], compare_op=ALU.is_ge, fill=0.0, base=0,
                               pattern=[[1, P]], channel_multiplier=-1).then_inc(consts, 1)
            pool.wait_ge(consts, 3)
            blocks = causal[:].rearrange("p (b q) -> p b q", q=S)
            pool.affine_select(out=blocks, in_=blocks, compare_op=ALU.is_ge, fill=0.0, base=0,
                               pattern=[[-S, P // S], [0, S]], channel_multiplier=1).then_inc(consts, 1)
            pool.wait_ge(consts, 4)
            for b in range(BT):
                r = slice(b * S, (b + 1) * S)
                pool.tensor_copy(seen[r], causal[r, r]).then_inc(consts, 1)
            pool.wait_ge(consts, 8)
            pool.wait_ge(bf_in, 16)
            pool.wait_ge(w_lo_done, 5)
            pool.memset(pr[0][:], 0.0).then_inc(pr_zero, 1)

            def add_bias(s):
                pool.wait_ge(xn3_done, s + 1)
                pool.tensor_tensor(res, res, bf[:].unsqueeze(1).to_broadcast([P, TILES, D]),
                                   ALU.add).then_inc(xb_done, 1)

            def step(s, prev=True, more=True):
                if prev:
                    add_bias(s - 1)
                    pool.wait_ge(t3_mm, s * 4)
                    pool.tensor_tensor(pool_gate[:], ones[0:1, 0:1], ones[0:1, 0:1], ALU.mult)
                pool.memset(xn3, 0.0).then_inc(pr_zero, 1)
                def o_low(t):
                    pool.wait_ge(o_hi, s * 4 + (t + 1))
                    pool.tensor_tensor(xt3_lo[:, :, t * P:(t + 1) * P], ot[:, t % 2],
                                       xt3_hi[:, :, t * P:(t + 1) * P].bitcast(F32), ALU.subtract).then_inc(o_lo, 1)

                for t in range(TILES):
                    pool.wait_ge(den_done, s * 16 + (4 * t + 4))
                    pool.wait_ge(o_raw, s * 4 + (t + 1))
                    o = ot[:, t % 2].rearrange("p c q -> p (c q)")
                    pool.tensor_tensor(o, o, rden[:, t % 2],
                                       ALU.mult).then_inc(o_done, 1)
                    o_low(t)

            steps(pool, step)
            for h in range(2):
                pool.wait_ge(xn3_done, LAST + (h + 1))
                half = res[:, 2 * h:2 * h + 2]
                pool.tensor_tensor(half, half, bf[:].unsqueeze(1).to_broadcast([P, 2, D]),
                                   ALU.add).then_inc(xb_done, 1)

        @block.scalar
        def _(act):
            def high(s, c, mm, hi_sem, hi, free, count):
                act.wait_ge(mm, s * 4 + (c + 1))
                if c == 0:
                    wait(act, free, count)
                act.copy(hi[:, c, :], ps[:, TRN[c % 2], :]).then_inc(hi_sem, 1)

            def step(s, prev=True, more=True):
                def evac(n):
                    act.wait_ge(qkv_mm, s * 12 + (n + 1))
                    bank = ps[:, PROJ[n % 2], :]
                    if n < 4:
                        if n == 0:
                            wait(act, pv_mm, s * 16)
                        if not prev:
                            act.wait_ge(zeroed, n + 1)
                        for j in range(HG):
                            r = slice(j * DK, (j + 1) * DK)
                            i = act.activation(qb[r, n, :, j * S:(j + 1) * S],
                                               bank[r].rearrange("p (u q) -> p u q", q=S), ACT.Copy, scale=SCALE)
                    elif n < 8:
                        i = act.copy(k[:, n - 4, :], bank)
                    else:
                        i = act.copy(v[:, n - 8, :], bank)
                    i.then_inc(qkv_evac, 1)

                def o_out(t):
                    act.wait_ge(pv_mm, s * 16 + (4 * t + 4))
                    wait(act, o_lo, s * 4 + (t - 1))
                    act.copy(ot[:, t % 2].rearrange("p c q -> p (c q)"), ps[:, OT[t % 2], :]).then_inc(o_raw, 1)

                def o_high(t):
                    act.wait_ge(o_done, s * 4 + (t + 1))
                    if t == 0:
                        wait(act, ffn_mm, s * 4)
                    act.copy(xt3_hi[:, :, t * P:(t + 1) * P], ot[:, t % 2]).then_inc(o_hi, 1)

                for n in range(12):
                    evac(n)
                    if prev and 0 <= n - TURN3 < C:
                        high(s - 1, n - TURN3, t3_mm, t3_hi, xt3_hi, out_mm, s * 4)
                    if not prev and n in (3, 7):
                        self_weight_high(act, w, 3 + (n == 7))
                if more:
                    for c in range(C - 1):
                        high(s + 1, c, t2_mm, t2_hi, xt2_hi, qkv_mm, s * 12 + 12)
                def exps(t):
                    act.wait_ge(sc_mm, s * 4 + (t + 1))
                    wait(act, pr_dve, s * 4 + t)
                    wait(act, pr_act, s * 12 + 3 * t)
                    act.activation(ex[:].rearrange("p h q -> p (h q)"), ps[:, SC[t % 2], :],
                                   ACT.Exp).then_inc(exp_done, 1)

                def spreads(t):
                    if t == 0:
                        act.wait_ge(pr_zero, s + 2)
                    act.wait_ge(clipped, s * 4 + (t + 1))
                    wait(act, pv_mm, s * 16 + (4 * t - 4))
                    for b in range(BT - 1):
                        spread(act.copy, b, t).then_inc(pr_act, 1)

                exps(0)
                spreads(0)
                if more:
                    high(s + 1, 3, t2_mm, t2_hi, xt2_hi, qkv_mm, s * 12 + 12)
                exps(1)
                spreads(1)
                exps(2)
                spreads(2)
                o_out(0)
                exps(3)
                spreads(3)
                o_out(1)
                o_high(0)
                o_out(2)
                o_high(1)
                o_out(3)
                o_high(2)
                o_high(3)

            for c in range(C):
                high(0, c, t2_mm, t2_hi, xt2_hi, None, 0)
            self_weight_high(act, w, 2)
            steps(act, step)
            act.wait_ge(out_mm, NSUP * 4)
            for h in range(2):
                for c in range(C):
                    act.wait_ge(t3_mm, (LAST + h) * 4 + (c + 1))
                    act.copy(xt3_hi[:, c, half_columns(h)], ps[:, TRN[c % 2], half_columns(h)]).then_inc(t3_hi, 1)

        @block.vector
        def _(dve):
            def ln2(s):
                dve.wait_ge(xl_in, s * 16 + 16)
                layer_norm(dve, xl, xl, w, xn2_done, step2, s * LN_STEPS)

            def ln3(s):
                dve.wait_ge(x3_done, s * 4 + 4)
                wait(dve, t3_mm, s * 4)
                layer_norm(dve, res, xn3, w, xn3_done, step3, s * LN_STEPS)

            def half_low(h):
                for c in range(C):
                    dve.wait_ge(t3_hi, (LAST + h) * 4 + (c + 1))
                    dve.tensor_tensor(xt3_lo[:, c, half_columns(h)], ps[:, TRN[c % 2], half_columns(h)],
                                      xt3_hi[:, c, half_columns(h)].bitcast(F32), ALU.subtract).then_inc(t3_lo, 1)

            def half_ln3(h):
                layer_norm(dve, res, xn3, w, xn3_done, step3, (LAST + h) * LN_STEPS, half_tiles(h))

            def low(s, c, hi_sem, lo_sem, hi, lo):
                dve.wait_ge(hi_sem, s * 4 + (c + 1))
                dve.tensor_tensor(lo[:, c, :], ps[:, TRN[c % 2], :], hi[:, c, :].bitcast(F32),
                                  ALU.subtract).then_inc(lo_sem, 1)

            def ffn_add(s, t):
                if t == 0:
                    dve.wait_ge(xb_done, s + 1)
                dve.wait_ge(ffn_mm, s * 4 + (t + 1))
                dve.tensor_tensor(res[:, t, :], ps[:, PROJ[t % 2], :], res[:, t, :], ALU.add).then_inc(y_done, 1)

            def step(s, prev=True, more=True):
                def divide(n):
                    t, g = n // 4, n % 4
                    if g == 0:
                        dve.wait_ge(pv_mm, s * 16 + (n + C))
                        wait(dve, o_done, s * 4 + (t - 1))
                    dve.reciprocal(rden[:, t % 2, g * P:(g + 1) * P],
                                   ps[:, DEN[t], g * P:(g + 1) * P]).then_inc(den_done, 1)
                def mask(t):
                    dve.wait_ge(exp_done, s * 4 + (t + 1))
                    dve.scalar_tensor_tensor(ex[:], ex[:], E_LOW, seen[:].unsqueeze(1).to_broadcast([P, H, S]),
                                             ALU.max, ALU.min).then_inc(clipped, 1)

                def spread_last(t):
                    if t == 0:
                        dve.wait_ge(pr_zero, s + 2)
                    dve.wait_ge(clipped, s * 4 + (t + 1))
                    wait(dve, pv_mm, s * 16 + (4 * t - 4))
                    spread(dve.tensor_copy, BT - 1, t).then_inc(pr_dve, 1)

                if prev:
                    ln3(s - 1)
                if more:
                    ln2(s + 1)
                if not prev:
                    self_weight_low(dve, w, 3)
                    self_weight_low(dve, w, 4)
                if prev:
                    for c in range(C):
                        low(s - 1, c, t3_hi, t3_lo, xt3_hi, xt3_lo)
                if not prev:
                    dve.wait_ge(consts, 8)
                for t in range(TILES):
                    if t == 3:
                        mask(0)
                        spread_last(0)
                    if prev:
                        ffn_add(s - 1, t)
                    if more:
                        low(s + 1, t, t2_hi, t2_lo, xt2_hi, xt2_lo)
                mask(1)
                spread_last(1)
                mask(2)
                spread_last(2)
                for n in range(16):
                    if n == 2:
                        mask(3)
                    if n == 4:
                        spread_last(3)
                    divide(n)
                dve.wait_ge(res_in, s * 16 + 16)
                for t in range(TILES):
                    dve.wait_ge(out_mm, s * 4 + (t + 1))
                    dve.tensor_tensor(res[:, t, :], ps[:, PROJ[t % 2], :], res[:, t, :],
                                      ALU.add).then_inc(x3_done, 1)
                    if t == 1 and not more:
                        dve.wait_ge(x3_done, s * 4 + 2)
                        wait(dve, t3_mm, s * 4)
                        half_ln3(0)

            for c in range(C):
                low(0, c, t2_hi, t2_lo, xt2_hi, xt2_lo)
            self_weight_low(dve, w, 2)
            steps(dve, step)
            half_low(0)
            dve.wait_ge(x3_done, NSUP * 4)
            half_ln3(1)
            for h in range(2):
                if h:
                    half_low(h)
                dve.wait_ge(xb_done, LAST + (h + 1))
                for t in half_tiles(h):
                    dve.wait_ge(ffn_mm, LAST * 4 + (t + 1))
                    dve.tensor_tensor(res[:, t, :], ps[:, PROJ[t % 2], :], res[:, t, :], ALU.add).then_inc(y_done, 1)

        @block.tensor
        def _(pe):
            def turn_chunk(s, c, x, ready, mm, lo_sem):
                if c == 0:
                    pe.wait_ge(ready, s + 1)
                if c >= 2:
                    wait(pe, lo_sem, s * 4 + (c - 1))
                for t in range(TILES):
                    i = pe.transpose(ps[:, TRN[c % 2], t * P:(t + 1) * P], x[:, t, c * P:(c + 1) * P],
                                     w["ident"][:])
                i.then_inc(mm, 1)

            def tile_product(s, t, x_hi, x_lo, n, mm, done, before, count):
                if t < 2:
                    pe.wait_ge(before, count + (t - 1))
                else:
                    pe.wait_ge(done, s * 4 + (t - 1))
                r = slice(t * P, (t + 1) * P)
                product3(pe, ps[:, PROJ[t % 2], :], lambda c: x_hi[:, c, r], lambda c: x_lo[:, c, r],
                         lambda c: w_hi[n][:, c, :], lambda c: w_lo[n][:, c, :]).then_inc(mm, 1)

            def step(s, prev=True, more=True):
                pe.wait_ge(t2_lo, s * 4 + 4)
                for n in range(12):
                    if not prev and n in (0, 8):
                        pe.wait_ge(w_lo_done, 2 + n // 8)
                    if n >= 2:
                        pe.wait_ge(qkv_evac, s * 12 + (n - 1))
                    else:
                        wait(pe, x3_done, s * 4 + (n - 1))
                    out = ps[:, PROJ[n % 2], :]
                    if n < 8:
                        r = slice((n % 4) * P, (n % 4 + 1) * P)
                        i = product3(pe, out, lambda c: w_hi[n // 4][:, c, r], lambda c: w_lo[n // 4][:, c, r],
                                     lambda c: xt2_hi[:, c, :], lambda c: xt2_lo[:, c, :])
                    else:
                        r = slice((n - 8) * P, (n - 7) * P)
                        i = product3(pe, out, lambda c: xt2_hi[:, c, r], lambda c: xt2_lo[:, c, r],
                                     lambda c: w_hi[2][:, c, :], lambda c: w_lo[2][:, c, :])
                    i.then_inc(qkv_mm, 1)
                    if prev and 0 <= n - TURN3 < C:
                        turn_chunk(s - 1, n - TURN3, xn3, xn3_done, t3_mm, t3_lo)

                def scores(t):
                    wait(pe, exp_done, s * 4 + (t - 1))
                    for g in range(C):
                        for b in range(BT):
                            i = pe.matmul(ps[b * S:(b + 1) * S, SC[t % 2], g * P:(g + 1) * P],
                                          k[:, g, t * P + b * S:t * P + (b + 1) * S], qb[:, g, t * BT + b, :],
                                          start=True, stop=True)
                    i.then_inc(sc_mm, 1)

                if prev:
                    pe.wait_ge(t3_lo, s * 4)
                for t in range(TILES):
                    if t == 3:
                        pe.wait_ge(qkv_evac, s * 12 + 12)
                        scores(0)
                    if prev:
                        tile_product(s - 1, t, xt3_hi, xt3_lo, 4, ffn_mm, y_done, qkv_evac, s * 12 + 12)
                    if more:
                        turn_chunk(s + 1, t, xl, xn2_done, t2_mm, t2_lo)

                def values(n):
                    t, g = n // 4, n % 4
                    if g == 0:
                        pe.wait_ge(pr_act, s * 12 + (3 * t + 3))
                        pe.wait_ge(pr_dve, s * 4 + (t + 1))
                        wait(pe, o_raw, s * 4 + (t - 1))
                        if t == 1 and more:
                            pe.wait_ge(t2_lo, s * 4 + 8)
                    for j in range(HG):
                        r = slice(j * DK, (j + 1) * DK)
                        m = pr[t % 2][:, g * HG + j, :]
                        pe.matmul(ps[r, OT[t % 2], g * P:(g + 1) * P],
                                  v[:, t, g * P + j * DK:g * P + (j + 1) * DK], m, start=True, stop=True)
                    for j in range(HG):
                        r = slice(j * DK, (j + 1) * DK)
                        m = pr[t % 2][:, g * HG + j, :]
                        i = pe.matmul(ps[r, DEN[t], g * P:(g + 1) * P], ones[:], m, start=True, stop=True)
                    i.then_inc(pv_mm, 1)

                if not prev:
                    pe.wait_ge(consts, 8)
                scores(1)
                for t in range(TILES):
                    if t + 2 < TILES:
                        scores(t + 2)
                    for g in range(C):
                        values(t * C + g)
                if not prev:
                    pe.wait_ge(w_lo_done, 5)
                for t in range(TILES):
                    pe.wait_ge(o_lo, s * 4 + (t + 1))
                    if prev:
                        tile_product(s, t, xt3_hi, xt3_lo, 3, out_mm, x3_done, y_done, s * 4)
                    else:
                        tile_product(s, t, xt3_hi, xt3_lo, 3, out_mm, x3_done, qkv_evac, s * 12 + 12)

            for c in range(C):
                turn_chunk(0, c, xl, xn2_done, t2_mm, t2_lo)
            steps(pe, step)
            for h in range(2):
                pe.wait_ge(xn3_done, LAST + (h + 1))
                for c in range(C):
                    wait(pe, t3_lo, (LAST + h) * 4 + (c - 1))
                    for t in half_tiles(h):
                        i = pe.transpose(ps[:, TRN[c % 2], t * P:(t + 1) * P], xn3[:, t, c * P:(c + 1) * P],
                                         w["ident"][:])
                    i.then_inc(t3_mm, 1)
                pe.wait_ge(t3_lo, (LAST + h) * 4 + 4)
                for t in half_tiles(h):
                    tile_product(LAST, t, xt3_hi, xt3_lo, 4, ffn_mm, y_done, x3_done, NSUP * 4)


def program(nc, io):
    scr_q = nc.dram_tensor("q_scratch", [PAIRS, P, C * 64], F32, kind="Internal").ap()
    scr_x2 = nc.dram_tensor("x2_scratch", [QUADS, P, D], F32, kind="Internal").ap()
    scr = {
        "q": scr_q.rearrange("(s a) p n -> s a p n", s=NSUP),
        "q_pairs": scr_q.rearrange("a p (g t) -> a p g t", g=C),
        "x2": scr_x2,
        "x2_sup": scr_x2.rearrange("(s t) p n -> s p t n", s=NSUP),
    }
    with ExitStack() as ctx:
        def sb(name, shape, dt=F32):
            return ctx.enter_context(nc.sbuf_tensor(name, shape, dt))

        def sem(name):
            return ctx.enter_context(nc.semaphore(name))

        w = {"ident": sb("ident", [P, P]), "choice": sb("choice", [1, OPS], U32),
             "split_hi": sb("split_hi", [P, 2, C, SUP], F32R), "split_lo": sb("split_lo", [P, 2, C, SUP], F32R),
             "stats": sb("stats", [P, TILES, 6]), "mv": sb("mv", [P, TILES, 2]),
             "small": sb("small", [P, 3, TILES]), "gate": sb("gate", [1, 1])}
        for name in ("wk", "wv", "wo"):
            for part in ("hi", "lo"):
                w[f"{name}_{part}"] = sb(f"{name}_{part}", [P, C, D], F32R)
        raw = sb("raw", [P, 2, 2 * C * KEYS])
        w["ctx"] = raw[:].rearrange("p a (h c k) -> p a h c k", h=2, c=C)
        w["xl"], w["res"] = (raw[:, k, 0:TILES * D].rearrange("p (t n) -> p t n", n=D) for k in range(2))
        w["c_hi"], w["c_lo"] = ((w[f"wk_{part}"][:], w[f"wv_{part}"][:]) for part in ("hi", "lo"))
        w["v"] = sb("v", [P, 2, 4, D])
        w["row"] = sb("row", [P, D])
        w["staging"] = (w["res"], w["v"][:, 0])
        for name in ("ident_ready", "cx_hi_done", "cx_done", "xl_in", "xn2_done", "ln2_step", "w_hi_done",
                     "w_lo_done", "x2_stored"):
            w[name] = sem(name)
        w["ctx_in"] = [sem("ctx_in0"), sem("ctx_in1")]
        w["q_stored"] = [sem("q_stored0"), sem("q_stored1")]
        w["w_in"] = [sem(f"w_in{n}") for n in range(5)]
        with ExitStack() as cross:
            w["v_last"] = cross.enter_context(nc.sbuf_tensor("v_last", [P, B, C], F32))
            w["bk"] = cross.enter_context(nc.sbuf_tensor("bk", [P, C], F32))
            phase_a(nc, io, w, scr)
            phase_b(nc, io, w, scr)
        phase_c(nc, io, w, scr)


def kernel(**inputs):
    import numpy as np
    import concourse.bacc as bacc
    from concourse.bass_utils import run_bass_kernel_spmd

    a = {n: np.asarray(v) for n, v in inputs.items()}
    ctx = a["ctx_1024"]
    arrays = {
        "x": a["x"].reshape(TOK, D),
        "ctx": ctx.reshape(B, KEYS, C, P).transpose(0, 3, 2, 1),
        "ctx_last": ctx[:, NK].reshape(B, C, P).transpose(2, 1, 0),
        "mask": a["mask_BxSxS2_ik0"].reshape(PAIRS, 2, S, KEYS).transpose(0, 2, 1, 3),
        "wqkv": a["L0_attn_Wqkv"].reshape(3, D, D).transpose(0, 2, 1),
        "wout": a["L0_attn_Wout"].T,
        "W": a["L0_ffn_W"], "b": a["L0_ffn_b"],
        "logits": a["L0_ffn_logits"].reshape(1, OPS), "u": a["L0_ffn_u"].reshape(1, OPS),
    }
    for n in ("Wq", "Wk", "Wv", "Wo"):
        arrays[n] = a["L0_xattn_" + n]
    for n in ("bq", "bk", "bv"):
        arrays[n] = a["L0_xattn_" + n].reshape(C, P).T
    arrays["bo"] = a["L0_xattn_bo"]
    arrays = {f"{n}_dram": np.ascontiguousarray(v) for n, v in arrays.items()}

    nc = bacc.Bacc("TRN2", target_bir_lowering=False, num_devices=1)
    t = {n[:-5]: nc.dram_tensor(n, v.shape, mybir.dt.from_np(v.dtype), kind="ExternalInput").ap()
         for n, v in arrays.items()}
    out = nc.dram_tensor("out_dram", (TOK, D), F32, kind="ExternalOutput").ap()
    io = dict(t)
    io["x"] = t["x"].rearrange("(s t p) n -> s t p n", s=NSUP, t=TILES)
    io["x_tiles"] = t["x"].rearrange("(k p) n -> k p n", p=P)
    io["out"] = out.rearrange("(s t p) n -> s p t n", s=NSUP, t=TILES)
    io["wqkv"] = t["wqkv"].rearrange("m (c p) n -> m p c n", p=P)
    io["W"] = t["W"].rearrange("m (c p) n -> m p c n", p=P)
    io["wout"] = t["wout"].rearrange("(c p) n -> p c n", p=P)
    for n in ("Wq", "Wk", "Wv", "Wo"):
        io[n] = t[n].rearrange("(c p) n -> p c n", p=P)
    program(nc, io)
    r = run_bass_kernel_spmd(nc, [arrays], core_ids=[0])
    return r.results[0]["out_dram"].reshape(B, S, D)
```
